# Optimizing a Trainium2 kernel written in Bass

```python
import numpy as np
import jax
import jax.numpy as jnp

def _softmax(x, axis=-1):
    return jax.nn.softmax(x, axis=axis)

def _gelu(x):
    return jax.nn.gelu(x, approximate=True)

def _silu(x):
    return jax.nn.silu(x)

def _sigmoid(x):
    return jax.nn.sigmoid(x)

def _layernorm(x, axis=-1, eps=1e-05):
    m = jnp.mean(x, axis=axis, keepdims=True)
    v = jnp.var(x, axis=axis, keepdims=True)
    return (x - m) / jnp.sqrt(v + eps)

def _scatter_add(tgt, idx, src, axis=0):
    return tgt.at[idx].add(src)

def _segment_sum(src, seg, n):
    return jax.ops.segment_sum(src, seg, n)
kernel_name = 'mk_seq_preln_d1_jaxref_r4_a0181b'

def setup_inputs(seed: int=0):
    np.random.seed(seed)
    _w = jnp.asarray

    def _L0_attn_setup():
        import jax, jax.numpy as jnp
        import numpy as np
        import math
        D_MODEL = 256
        NUM_HEADS = 16
        D_K = D_MODEL // NUM_HEADS
        THETA = 10000.0
        MAX_SEQ_LEN = 512
        B, S = (2, 512)

        def _trunc_normal(key, shape, std):
            x = jax.random.normal(key, shape, dtype=jnp.float32) * std
            return jnp.clip(x, -3.0 * std, 3.0 * std)

        def _rope(x):
            seq_len, d_k = (x.shape[-2], x.shape[-1])
            freqs = 1.0 / THETA ** (jnp.arange(0, d_k, 2, dtype=jnp.float32) / d_k)
            angles = jnp.arange(seq_len, dtype=jnp.float32)[:, None] * freqs[None, :]
            cos, sin = (jnp.cos(angles), jnp.sin(angles))
            x_even, x_odd = (x[..., 0::2], x[..., 1::2])
            x_even_rot = x_even * cos - x_odd * sin
            x_odd_rot = x_even * sin + x_odd * cos
            out = jnp.stack([x_even_rot, x_odd_rot], axis=-1)
            return out.reshape(x.shape)
        key = jax.random.key(seed)
        kx, kq, kk, kv, ko = jax.random.split(key, 5)
        std = math.sqrt(2.0 / (D_MODEL + D_MODEL))
        return {'x': jax.random.normal(kx, (B, S, D_MODEL), dtype=jnp.float32), 'Wq': _trunc_normal(kq, (D_MODEL, D_MODEL), std), 'Wk': _trunc_normal(kk, (D_MODEL, D_MODEL), std), 'Wv': _trunc_normal(kv, (D_MODEL, D_MODEL), std), 'Wo': _trunc_normal(ko, (D_MODEL, D_MODEL), std)}
    _L0_attn_in = _L0_attn_setup()

    def _L0_ffn_setup():
        import jax, jax.numpy as jnp
        import numpy as np
        B, S, D = (4, 512, 256)
        N_EXPERTS, EXPERT_SIZE = (16, 64)
        WIDTH = N_EXPERTS * EXPERT_SIZE
        key = jax.random.key(seed)
        k_x, k_w1, k_w2, k_g = jax.random.split(key, 4)
        x = jax.random.normal(k_x, (B, S, D), dtype=jnp.float32)
        w1 = jax.random.normal(k_w1, (D, WIDTH), dtype=jnp.float32) / np.sqrt(D).astype(np.float32)
        b1 = jnp.zeros((WIDTH,), dtype=jnp.float32)
        w2 = jax.random.normal(k_w2, (WIDTH, D), dtype=jnp.float32) / np.sqrt(WIDTH).astype(np.float32)
        b2 = jnp.zeros((D,), dtype=jnp.float32)
        return {'x': x, 'w1': w1, 'b1': b1, 'w2': w2, 'b2': b2}
    _L0_ffn_in = _L0_ffn_setup()
    _d = {'L0_attn_x': _L0_attn_in['x'], 'L0_attn_Wq': _L0_attn_in['Wq'], 'L0_attn_Wk': _L0_attn_in['Wk'], 'L0_attn_Wv': _L0_attn_in['Wv'], 'L0_attn_Wo': _L0_attn_in['Wo'], 'L0_ffn_w1': _L0_ffn_in['w1'], 'L0_ffn_b1': _L0_ffn_in['b1'], 'L0_ffn_w2': _L0_ffn_in['w2'], 'L0_ffn_b2': _L0_ffn_in['b2']}
    _x0 = _d['L0_attn_x']
    _d['L0_attn_x'] = jax.random.normal(jax.random.fold_in(jax.random.key(seed), 1), (4, 2048, 256), dtype=_x0.dtype)
    del _x0
    return _d

def reference(L0_attn_x, L0_attn_Wq, L0_attn_Wk, L0_attn_Wv, L0_attn_Wo, L0_ffn_w1, L0_ffn_b1, L0_ffn_w2, L0_ffn_b2):

    def _L0_attn_ref(x, Wq, Wk, Wv, Wo):
        import jax, jax.numpy as jnp
        import numpy as np
        import math
        D_MODEL = 256
        NUM_HEADS = 16
        D_K = D_MODEL // NUM_HEADS
        THETA = 10000.0
        MAX_SEQ_LEN = 512
        B, S = (2, 512)

        def _trunc_normal(key, shape, std):
            x = jax.random.normal(key, shape, dtype=jnp.float32) * std
            return jnp.clip(x, -3.0 * std, 3.0 * std)

        def _rope(x):
            seq_len, d_k = (x.shape[-2], x.shape[-1])
            freqs = 1.0 / THETA ** (jnp.arange(0, d_k, 2, dtype=jnp.float32) / d_k)
            angles = jnp.arange(seq_len, dtype=jnp.float32)[:, None] * freqs[None, :]
            cos, sin = (jnp.cos(angles), jnp.sin(angles))
            x_even, x_odd = (x[..., 0::2], x[..., 1::2])
            x_even_rot = x_even * cos - x_odd * sin
            x_odd_rot = x_even * sin + x_odd * cos
            out = jnp.stack([x_even_rot, x_odd_rot], axis=-1)
            return out.reshape(x.shape)
        b, s, d = x.shape
        Q = jnp.einsum('bsd,ed->bse', x, Wq).reshape(b, s, NUM_HEADS, D_K).transpose(0, 2, 1, 3)
        K = jnp.einsum('bsd,ed->bse', x, Wk).reshape(b, s, NUM_HEADS, D_K).transpose(0, 2, 1, 3)
        V = jnp.einsum('bsd,ed->bse', x, Wv).reshape(b, s, NUM_HEADS, D_K).transpose(0, 2, 1, 3)
        Q = _rope(Q)
        K = _rope(K)
        scores = jnp.einsum('bhqd,bhkd->bhqk', Q, K) / math.sqrt(D_K)
        causal_mask = jnp.triu(jnp.ones((s, s), dtype=bool), k=1)
        scores = jnp.where(causal_mask[None, None], -jnp.inf, scores)
        attn = jax.nn.softmax(scores, axis=-1)
        out = jnp.einsum('bhqk,bhkd->bhqd', attn, V)
        out = out.transpose(0, 2, 1, 3).reshape(b, s, d)
        return jnp.einsum('bsd,ed->bse', out, Wo)

    def _L0_ffn_ref(x, w1, b1, w2, b2):
        import jax, jax.numpy as jnp
        import numpy as np
        B, S, D = (4, 512, 256)
        N_EXPERTS, EXPERT_SIZE = (16, 64)
        WIDTH = N_EXPERTS * EXPERT_SIZE
        h = jax.nn.relu(jnp.einsum('bsd,dw->bsw', x, w1) + b1)
        return jnp.einsum('bsw,wd->bsd', h, w2) + b2
    x = L0_attn_x
    x = x + _L0_attn_ref(_layernorm(x, axis=-1), L0_attn_Wq, L0_attn_Wk, L0_attn_Wv, L0_attn_Wo)
    x = x + _L0_ffn_ref(_layernorm(x, axis=-1), L0_ffn_w1, L0_ffn_b1, L0_ffn_w2, L0_ffn_b2)
    return x

_drawn_inputs = setup_inputs


def setup_inputs(seed=0):
    import zlib

    import numpy as np

    out = dict(_drawn_inputs(seed))
    spreads = {'L0_ffn_b1': (0.0, 0.1), 'L0_ffn_b2': (0.0, 0.1)}
    factors = {}
    for name, (base, spread) in spreads.items():
        noise = np.random.default_rng([zlib.crc32(name.encode()), seed]).standard_normal(out[name].shape)
        drawn = base * np.exp(spread * noise) if base else spread * noise
        out[name] = jnp.asarray(drawn.astype(out[name].dtype))
    for name, factor in factors.items():
        out[name] = (out[name] * factor).astype(out[name].dtype)
    return out
```

```python
from contextlib import ExitStack

import numpy as np

import concourse.bass as bass
from concourse import mybir

ALU = mybir.AluOpType
ACT = mybir.ActivationFunctionType
AX = mybir.AxisListType
F32 = mybir.dt.float32
F16 = mybir.dt.float16

P = 128
B, S, D, H, F = 4, 2048, 256, 16, 1024
DK = D // H
CH = 512
NC = S // CH
TPC = CH // P
NCHUNK = B * NC
KD = D // P
KF = F // P
G = 4
NG = H // G
GC = G * DK
NIT = B * NG
EPS = 1e-5

SX = 64.0
SH = 16.0
SQK = SX * SX

ROLE_ROWS = 3 * DK
MAXROW = ROLE_ROWS
HROWS = 64
MROWS = 32 * (G - 1) + DK
AROWS = HROWS + MAXROW + 1

STEPS = [(c, kb) for c in range(NC) for kb in range(TPC * (c + 1))]
NS = len(STEPS)
CHUNK_END = [max(s for s in range(NS) if STEPS[s][0] == c) for c in range(NC)]
HALF_STEP = CHUNK_END[NC // 2 - 1] + 1
UNITS = G * NS
NDIAG = NC * TPC
MASKED = -1e30


def is_diagonal(s):
    c, kb = STEPS[s]
    return kb >= TPC * c


def diagonals(s):
    return sum(is_diagonal(t) for t in range(s))


def terms(a_hi, a_lo, b_hi, b_lo):
    return ((a_hi, b_hi), (a_hi, b_lo), (a_lo, b_hi))


def stage1(nc, x, w_qkv, cos_d, sin_d, ident_d, qk_d, v_d):
    with ExitStack() as ctx:
        def sb(name, shape, dt):
            return ctx.enter_context(nc.sbuf_tensor(name, shape, dt))

        def sem(name):
            return ctx.enter_context(nc.semaphore(name))

        NW = 3 * D
        w_f = sb("s1_w_f", [P, KD, NW], F32)
        w_hi = sb("s1_w_hi", [P, KD, NW], F16)
        w_lo = sb("s1_w_lo", [P, KD, NW], F16)
        cos = sb("s1_cos", [P, S], F32)
        sin = sb("s1_sin", [P, S], F32)
        ident = sb("s1_ident", [P, P], F32)
        eps = sb("s1_eps", [P, 1], F32)
        xin = sb("s1_xin", [P, 2, TPC, D], F32)
        xn = sb("s1_xn", [P, 2, TPC, D], F32)
        stats = sb("s1_stats", [P, 2, TPC, 6], F32)
        mv = sb("s1_mv", [P, 2, TPC, 2], F32)
        std = sb("s1_std", [P, 2, TPC], F32)
        rstd = sb("s1_rstd", [P, 2, TPC], F32)
        xt_hi = sb("s1_xt_hi", [P, 2, KD, CH], F16)
        xt_lo = sb("s1_xt_lo", [P, 2, KD, CH], F16)
        rot_a = sb("s1_rot_a", [P, NG, CH], F32)
        rot_b = sb("s1_rot_b", [P, NG, CH], F32)
        r_hi = sb("s1_r_hi", [P, NG, CH], F16)
        r_lo = sb("s1_r_lo", [P, NG, CH], F16)
        vst = sb("s1_vst", [P, 2, TPC, H, 2 * DK], F32)
        ps = ctx.enter_context(nc.psum_tensor("s1_ps", [P, 8, CH], F32))
        XT_BANK, QK_BANK, V_BANK = 0, 2, 6

        const_in = sem("s1_const_in")
        whi_done, w_done, preset = sem("s1_whi_done"), sem("s1_w_done"), sem("s1_preset")
        x_in = [sem(f"s1_x_in{p}") for p in range(2)]
        stats_done, mv_done, std_done = sem("s1_stats_done"), sem("s1_mv_done"), sem("s1_std_done")
        rstd_done, xn_done = sem("s1_rstd_done"), sem("s1_xn_done")
        xt_ready, xhi_done, xlo_done = sem("s1_xt_ready"), sem("s1_xhi_done"), sem("s1_xlo_done")
        qk_ready, v_ready = sem("s1_qk_ready"), sem("s1_v_ready")
        rot_read, rotsin_done, rot_done = sem("s1_rot_read"), sem("s1_rotsin_done"), sem("s1_rot_done")
        rhi_done, rlo_done = sem("s1_rhi_done"), sem("s1_rlo_done")
        v_copied = sem("s1_v_copied")
        qk_out = [sem(f"s1_qk_out{g}") for g in range(NG)]
        v_out = [sem(f"s1_v_out{p}") for p in range(2)]

        block = ctx.enter_context(nc.Block())

        @block.sync
        def _(sp):
            def load_x(n, p):
                sp.dma_start(xin[:, p], x[bass.ds(n * CH, CH), :].rearrange("(t p) d -> p t d", p=P)
                             ).then_inc(x_in[p], 16)

            for g in range(NG):
                sp.sem_inc(qk_out[g], 32)
            for p in range(2):
                sp.sem_inc(v_out[p], 16)
            load_x(0, 0)
            for dst, src in ((ident[:], ident_d), (w_f[:], w_qkv.rearrange("(k p) n -> p k n", p=P)),
                             (cos[:], cos_d), (sin[:], sin_d)):
                sp.dma_start(dst, src).then_inc(const_in, 16)
            load_x(1, 1)

            def chunks(b, last):
                for cc in range(NC):
                    n = NC * b + cc
                    for g in range(NG):
                        sp.wait_ge(rlo_done, NG * (n + 1) + g + 1)
                        for hl, src in ((1, r_lo), (0, r_hi)):
                            dst = qk_d[bass.ds(NG * b + g, 1), :, hl, :, cc * CH:(cc + 1) * CH].rearrange(
                                "a q r t -> (a q) r t")
                            sp.dma_start(dst, src[:, g, :]).then_inc(qk_out[g], 16)
                        if g == 0 and not (last and cc >= NC - 2):
                            sp.wait_ge(xn_done, n + 1)
                            load_x(n + 2, cc % 2)
                    sp.wait_ge(v_copied, 2 * (n + 1) + 2)
                    dst = v_d[:, TPC * cc:TPC * (cc + 1), bass.ds(NG * b, NG), :].rearrange("p t g n -> p t (g n)")
                    src = vst[:, cc % 2].rearrange("p t h e -> p t (h e)")
                    sp.dma_start(dst, src).then_inc(v_out[cc % 2], 16)

            with sp.Fori(0, B - 1) as b:
                chunks(b, False)
            chunks(B - 1, True)
            for g in range(NG):
                sp.wait_ge(qk_out[g], 32 * (NCHUNK + 1))
            for p in range(2):
                sp.wait_ge(v_out[p], 16 * (NCHUNK // 2 + 1))

        @block.tensor
        def _(pe):
            def transposes(n, p):
                pe.wait_ge(xn_done, n + 1)
                pe.wait_ge(xlo_done, n)
                for k in range(KD):
                    for t in range(TPC):
                        last = nc.tensor.transpose(ps[:, XT_BANK + k, t * P:(t + 1) * P],
                                                   xn[:, p, t, k * P:(k + 1) * P], ident[:])
                last.then_inc(xt_ready, 1)

            def project_qk(n, p, g):
                pe.wait_ge(rot_read, NG * n + g + 1)
                mm = [(w, xt, k) for w, xt in terms(w_hi, w_lo, xt_hi, xt_lo) for k in range(KD)]
                for q, (w, xt, k) in enumerate(mm):
                    last = nc.tensor.matmul(ps[:, QK_BANK + g], w[:, k, 2 * GC * g:2 * GC * (g + 1)], xt[:, p, k],
                                            start=q == 0, stop=q == len(mm) - 1)
                last.then_inc(qk_ready, 1)

            def project_v(n, p):
                for pair in range(2):
                    pe.wait_ge(v_copied, 2 * n + pair + 1)
                    for t in range(2):
                        mm = [(xt, w, k) for xt, w in terms(xt_hi, xt_lo, w_hi, w_lo) for k in range(KD)]
                        for q, (xt, w, k) in enumerate(mm):
                            tt = 2 * pair + t
                            last = nc.tensor.matmul(ps[:, V_BANK + pair, t * D:(t + 1) * D],
                                                    xt[:, p, k, tt * P:(tt + 1) * P], w[:, k, 2 * D:3 * D],
                                                    start=q == 0, stop=q == len(mm) - 1)
                    last.then_inc(v_ready, 1)

            def chunks(b, last):
                for cc in range(NC):
                    n, p = NC * b + cc, cc % 2
                    pe.wait_ge(xlo_done, n + 1)
                    project_qk(n, p, 0)
                    project_qk(n, p, 1)
                    if not (last and cc == NC - 1):
                        transposes(n + 1, 1 - p)
                    project_qk(n, p, 2)
                    project_qk(n, p, 3)
                    project_v(n, p)

            pe.wait_ge(const_in, 64)
            transposes(0, 0)
            pe.wait_ge(w_done, 1)
            with pe.Fori(0, B - 1) as b:
                chunks(b, False)
            chunks(B - 1, True)

        @block.vector
        def _(dve):
            def statistics(n, p, use):
                dve.wait_ge(x_in[p], 16 * (use + 1))
                for t in range(TPC):
                    nc.vector.bn_stats(stats[:, p, t, :], xin[:, p, t, :]).then_inc(stats_done, 1)

            def normalize(n, p):
                for t in range(TPC):
                    last = nc.vector.bn_aggr(mv[:, p, t, :], stats[:, p, t, :])
                last.then_inc(mv_done, 1)
                dve.wait_ge(std_done, n + 1)
                nc.vector.reciprocal(rstd[:, p, :], std[:, p, :]).then_inc(rstd_done, 1)
                dve.wait_ge(rstd_done, n + 1)
                if not isinstance(n, int) or n > 1:
                    dve.wait_ge(xt_ready, n)
                for t in range(TPC):
                    last = nc.vector.tensor_scalar(xn[:, p, t, :], xin[:, p, t, :], mv[:, p, t, 0:1],
                                                   rstd[:, p, t:t + 1], ALU.subtract, ALU.mult)
                last.then_inc(xn_done, 1)

            def split_xt(n, p):
                dve.wait_ge(xhi_done, n + 1)
                for k in range(KD):
                    last = nc.vector.tensor_tensor(xt_lo[:, p, k], ps[:, XT_BANK + k], xt_hi[:, p, k], ALU.subtract)
                last.then_inc(xlo_done, 1)

            def rope(n, cc, g):
                tok = slice(cc * CH, (cc + 1) * CH)
                dve.wait_ge(qk_ready, NG * n + g + 1)
                dve.wait_ge(rlo_done, NG * n + g + 1)
                nc.vector.tensor_tensor(rot_a[:, g], ps[:, QK_BANK + g], cos[:, tok], ALU.mult)
                nc.vector.stream_shuffle(rot_b[:, g], ps[:, QK_BANK + g], [r ^ 1 for r in range(32)]
                                         ).then_inc(rot_read, 1)

            def split_rot(n, g):
                dve.wait_ge(rhi_done, NG * n + g + 1)
                nc.vector.tensor_tensor(r_lo[:, g], rot_a[:, g], r_hi[:, g], ALU.subtract).then_inc(rlo_done, 1)

            def chunks(b, last):
                for cc in range(NC):
                    n, p = NC * b + cc, cc % 2
                    more = not (last and cc == NC - 1)
                    if more:
                        statistics(n + 1, 1 - p, (2 * b + (cc + 1) // 2))
                        dve.wait_ge(stats_done, TPC * (n + 2))
                    rope(n, cc, 0)
                    if more:
                        normalize(n + 1, 1 - p)
                    rope(n, cc, 1)
                    split_rot(n, 0)
                    if more:
                        split_xt(n + 1, 1 - p)
                    rope(n, cc, 2)
                    split_rot(n, 1)
                    rope(n, cc, 3)
                    split_rot(n, 2)
                    split_rot(n, 3)

            dve.sem_inc(rot_read, NG)
            dve.sem_inc(rlo_done, NG)
            nc.vector.memset(eps[:], EPS / SX ** 2).then_inc(preset, 1)
            nc.vector.memset(vst[:], 1.0 / SX).then_inc(preset, 1)
            statistics(0, 0, 0)
            dve.wait_ge(stats_done, TPC)
            normalize(0, 0)
            split_xt(0, 0)
            dve.wait_ge(whi_done, 1)
            nc.vector.scalar_tensor_tensor(w_lo[:].rearrange("p k n -> p (k n)"), w_f[:].rearrange("p k n -> p (k n)"),
                                           SX, w_hi[:].rearrange("p k n -> p (k n)"), ALU.mult, ALU.subtract
                                           ).then_inc(w_done, 1)
            with dve.Fori(0, B - 1) as b:
                chunks(b, False)
            chunks(B - 1, True)

        @block.gpsimd
        def _(pool):
            pool.wait_ge(const_in, 64)
            with pool.Fori(0, B) as b:
                for cc in range(NC):
                    for g in range(NG):
                        u = NG * (NC * b + cc) + g
                        tok = slice(cc * CH, (cc + 1) * CH)
                        pool.wait_ge(rot_read, u + 1 + NG)
                        nc.gpsimd.tensor_tensor(rot_b[:, g], rot_b[:, g], sin[:, tok], ALU.mult).then_inc(rotsin_done, 1)
                        pool.wait_ge(rotsin_done, u + 1)
                        nc.gpsimd.tensor_tensor(rot_a[:, g], rot_a[:, g], rot_b[:, g], ALU.add).then_inc(rot_done, 1)

        @block.scalar
        def _(act):
            def std_of(n, p):
                act.wait_ge(mv_done, n + 1)
                nc.scalar.activation(std[:, p, :], mv[:, p, :, 1], ACT.Sqrt, bias=eps[:], scale=1.0 / SX ** 2
                                     ).then_inc(std_done, 1)

            def hi_xt(n, p):
                act.wait_ge(xt_ready, n + 1)
                for k in range(KD):
                    last = nc.scalar.copy(xt_hi[:, p, k], ps[:, XT_BANK + k])
                last.then_inc(xhi_done, 1)

            def hi_rot(n, b, g):
                act.wait_ge(rot_done, NG * n + g + 1)
                act.wait_ge(qk_out[g], 32 * (n + 1))
                nc.scalar.copy(r_hi[:, g], rot_a[:, g]).then_inc(rhi_done, 1)

            def stage_v(n, b, cc, pair):
                act.wait_ge(v_ready, 2 * n + pair + 1)
                act.wait_ge(v_out[cc % 2], 16 * (2 * b + cc // 2 + 1))
                nc.scalar.activation(vst[:, cc % 2, 2 * pair:2 * pair + 2, :, 0:DK],
                                     ps[:, V_BANK + pair].rearrange("p (t h e) -> p t h e", t=2, e=DK),
                                     ACT.Copy, scale=1.0 / SQK).then_inc(v_copied, 1)

            def chunks(b, last):
                for cc in range(NC):
                    n, p = NC * b + cc, cc % 2
                    more = not (last and cc == NC - 1)
                    if more:
                        std_of(n + 1, 1 - p)
                    hi_rot(n, b, 0)
                    if more:
                        hi_xt(n + 1, 1 - p)
                    for g in range(1, NG):
                        hi_rot(n, b, g)
                    for pair in range(2):
                        stage_v(n, b, cc, pair)

            act.sem_inc(v_copied, 2)
            act.wait_ge(preset, 2)
            std_of(0, 0)
            hi_xt(0, 0)
            act.wait_ge(const_in, 64)
            nc.scalar.activation(w_hi[:], w_f[:], ACT.Copy, scale=SX).then_inc(whi_done, 1)
            with act.Fori(0, B - 1) as b:
                chunks(b, False)
            chunks(B - 1, True)


def stage2(nc, ident_d, mask_d, qk_d, v_d, att_d, weight_ds, weights):
    with ExitStack() as ctx:
        def sb(name, shape, dt):
            return ctx.enter_context(nc.sbuf_tensor(name, shape, dt))

        def sem(name):
            return ctx.enter_context(nc.semaphore(name))

        ident = sb("s2_ident", [P, P], F32)
        mask = sb("s2_mask", [P, CH], F32)
        masked = sb("s2_masked", [P, G, CH], F32)
        mq = sb("s2_mq", [P, 2, G, S], F16)
        mk = sb("s2_mk", [P, 2, S], F16)
        aq = sb("s2_aq", [P, 2, G, S], F16)
        ak = sb("s2_ak", [P, 2, G // 2, S], F16)
        v = sb("s2_v", [P, 2, S // P, G, 2 * DK], F32)
        part = sb("s2_part", [P, 2, G, 8, NC], F32)
        qmax = sb("s2_qmax", [P, 2, G * 8], F32)
        nrow = sb("s2_nrow", [G * 8, 2, P], F16)
        prob = sb("s2_prob", [P, 2, G, CH], F32)
        o_sb = sb("s2_o", [P, 2, CH], F32)
        ot = sb("s2_ot", [P, 2, CH // 32, 32], F32)
        rsum = sb("s2_rsum", [P, 2, CH // 32], F32)
        yt = sb("s2_yt", [P, 2, CH // 32, 32], F32)
        y_sb = sb("s2_y", [P, 2, CH], F32)
        y_hi = sb("s2_y_hi", [P, 2, CH], F16)
        y_lo = sb("s2_y_lo", [P, 2, CH], F16)
        w_f = [sb(f"s2_w{q}_f", hi.shape, F32) for q, (hi, lo) in enumerate(weights)]
        ps = ctx.enter_context(nc.psum_tensor("s2_ps", [P, 8, CH], F32))
        M_BANK, NM, S_BANK, O_BANK = 0, 3, 3, 7
        A_DMAS = 2 * 3 * 2 + 1

        const_in = sem("s2_const_in")
        m_preset, a_preset, part_preset = sem("s2_m_preset"), sem("s2_a_preset"), sem("s2_part_preset")
        m_in = [sem(f"s2_m_in{p}") for p in range(2)]
        a_in = [sem(f"s2_a_in{p}") for p in range(2)]
        m_ready, m_read = sem("s2_m_ready"), sem("s2_m_read")
        qmax_done = sem("s2_qmax_done")
        w_in, w_scaled, whi_done, w_done = sem("s2_w_in"), sem("s2_w_scaled"), sem("s2_whi_done"), sem("s2_w_done")
        masking, selecting = sem("s2_masking"), sem("s2_selecting")
        rows_in = [sem(f"s2_rows_in{h}") for h in range(2)]
        s_ready, p_done, mask_done = sem("s2_s_ready"), sem("s2_p_done"), sem("s2_mask_done")
        pv_done, o_copied = sem("s2_pv_done"), sem("s2_o_copied")
        ot_done, rsum_done, yt_done = sem("s2_ot_done"), sem("s2_rsum_done"), sem("s2_yt_done")
        y_done, yhi_done, ylo_done = sem("s2_y_done"), sem("s2_yhi_done"), sem("s2_ylo_done")
        y_out = [sem(f"s2_y_out{p}") for p in range(2)]

        M_BEFORE, M_ITER = UNITS + 1, UNITS + 2
        ROWS2_STEP, ROWS1_STEP = 1, HALF_STEP + 1
        ST = G * NS

        def m_use(i, s, j):
            return M_BEFORE + i * M_ITER + G * s + j + (s > ROWS2_STEP) + (s > ROWS1_STEP)

        def rows_use(i, half):
            s = (ROWS1_STEP, ROWS2_STEP)[half]
            return M_BEFORE + i * M_ITER + G * (s + 1) + (half == 0)

        def bank_of(local):
            return M_BANK + (M_BEFORE + local) % NM

        assert M_ITER % NM == 0
        def m_bank(s, j):
            return bank_of(G * s + j + (s > ROWS2_STEP) + (s > ROWS1_STEP))

        def rows_bank(half):
            s = (ROWS1_STEP, ROWS2_STEP)[half]
            return bank_of(G * (s + 1) + (half == 0))

        def second_rows_use(i, last):
            return M_BEFORE + i * M_ITER if last else rows_use(i, 1)

        def second_rows_bank(last):
            return bank_of(0) if last else rows_bank(1)

        def qtile(s):
            c, kb = STEPS[s]
            return TPC * c + kb // (c + 1), kb % (c + 1)

        block = ctx.enter_context(nc.Block())

        @block.sync
        def _(sp):
            def load_m(i, p):
                for j in range(G):
                    rows = slice(32 * j, 32 * j + DK)
                    for qk, dst in ((0, mq[rows, p, j]), (1, mk[rows, p])):
                        src = qk_d[bass.ds(i, 1), qk, 0, DK * j:DK * (j + 1), :].rearrange("a r t -> (a r) t")
                        sp.dma_start(dst, src).then_inc(m_in[p], 16)

            def load_a(i, p):
                for qk, roles in ((0, (0, 1, 0)), (1, (0, 0, 1))):
                    for r, hl in enumerate(roles):
                        for jj in range(2):
                            rows = slice(HROWS * jj + DK * r, HROWS * jj + DK * (r + 1))
                            dst = ak[rows, p] if qk else aq[rows, p, jj:G:2]
                            src = qk_d[bass.ds(i, 1), qk, hl].rearrange("a (jp jj r) t -> (a jj) r jp t", jj=2, r=DK)
                            sp.dma_start(dst, src[jj]).then_inc(a_in[p], 16)
                sp.dma_start(v[:, p].rearrange("p k j e -> p k (j e)"),
                             v_d[:, :, bass.ds(i, 1), :].rearrange("p k a n -> p k (a n)")).then_inc(a_in[p], 16)

            def rows(i, p, half, use):
                sp.wait_ge(m_read, NM + use + 1)
                for j in range(G):
                    row = HROWS * (j % 2) + MAXROW
                    sp.dma_start(aq[row:row + 1, p, j, half * S // 2:(half + 1) * S // 2],
                                 nrow[8 * j:8 * j + 8, half, :]).then_inc(rows_in[half], 16)

            def store(i, c):
                sp.wait_ge(ylo_done, NC * i + c + 1 + 2)
                for hl, src in ((1, y_lo), (0, y_hi)):
                    dst = att_d[hl, bass.ds(i, 1), :, c * CH:(c + 1) * CH].rearrange("a p t -> (a p) t")
                    sp.dma_start(dst, src[:, c % 2]).then_inc(y_out[c % 2], 16)

            def iteration(i, p, first=False, last=False, load2=True):
                if load2:
                    sp.wait_ge(m_ready, M_BEFORE + i * M_ITER)
                    load_m(i + 2, p)
                rows(i, p, 1, second_rows_use(i, last))
                if not first:
                    store(i - 1, NC - 1)
                if not last:
                    if not first:
                        sp.wait_ge(pv_done, NS * i + 2)
                    load_a(i + 1, 1 - p)
                store(i, 0)
                if not last:
                    rows(i + 1, 1 - p, 0, rows_use(i, 0))
                store(i, 1)
                store(i, 2)

            sp.wait_ge(m_preset, 3)
            load_m(0, 0)
            sp.dma_start(ident[:], ident_d).then_inc(const_in, 16)
            sp.dma_start(mask[:], mask_d).then_inc(const_in, 16)
            load_m(1, 1)
            sp.wait_ge(a_preset, 2)
            load_a(0, 0)
            for dst, src in zip(w_f, weight_ds):
                sp.dma_start(dst[:], src.rearrange("(k p) n -> p k n", p=P)).then_inc(w_in, 16)
            rows(0, 0, 0, M_BEFORE - 1)
            iteration(0, 0, first=True)
            with sp.Fori(1, NIT - 3, 2) as i:
                iteration(i, 1)
                iteration(i + 1, 0)
            iteration(NIT - 3, 1)
            iteration(NIT - 2, 0, load2=False)
            iteration(NIT - 1, 1, last=True, load2=False)
            store(NIT - 1, NC - 1)
            for p in range(2):
                sp.wait_ge(y_out[p], 16 * 2 * NIT * NC // 2)

        @block.tensor
        def _(pe):
            def max_tile(p, s, j, use, bank):
                qt, kc = qtile(s)
                w = min(CH, (qt + 1) * P - kc * CH)
                pe.wait_ge(m_read, use + 1)
                nc.tensor.matmul(ps[:, bank, 0:w], mq[0:MROWS, p, j, qt * P:(qt + 1) * P],
                                 mk[0:MROWS, p, kc * CH:kc * CH + w], start=True, stop=True).then_inc(m_ready, 1)

            def max_rows(half, use, bank, qmax_count):
                pe.wait_ge(qmax_done, qmax_count)
                pe.wait_ge(m_read, use + 1)
                nc.tensor.transpose(ps[0:G * 8, bank, 0:P], qmax[:, half, :], ident[:]).then_inc(m_ready, 1)

            def score_tile(i, p, s, j):
                c, kb = STEPS[s]
                q0 = max(0, kb - TPC * c) * P
                pe.wait_ge(p_done, ST * i + G * s + j + 1)
                nc.tensor.matmul(ps[:, S_BANK + j, q0:CH], ak[0:AROWS, p, j // 2, kb * P:(kb + 1) * P],
                                 aq[0:AROWS, p, j, c * CH + q0:(c + 1) * CH], start=True, stop=True
                                 ).then_inc(s_ready, 1)

            def pv_step(i, p, s):
                c, kb = STEPS[s]
                q0 = max(0, kb - TPC * c) * P
                if kb == 0:
                    pe.wait_ge(o_copied, NC * i + c)
                if is_diagonal(s):
                    pe.wait_ge(mask_done, NDIAG * i + diagonals(s) + 1)
                else:
                    pe.wait_ge(p_done, ST * i + G * s + G + G)
                for j in range(G):
                    last = nc.tensor.matmul(ps[32 * j:32 * j + 32, O_BANK, q0:CH], v[:, p, kb, j, :],
                                            prob[:, s % 2, j, q0:CH], start=kb == 0, stop=kb == TPC * (c + 1) - 1)
                last.then_inc(pv_done, 1)

            def iteration(i, p, use, first=False, last=False):
                pe.wait_ge(a_in[p], A_DMAS * 16 * (use + 1))
                pe.wait_ge(rows_in[0], 16 * G * (i + 1))
                for s in range(NS):
                    if s == HALF_STEP:
                        pe.wait_ge(rows_in[1], 16 * G * (i + 1))
                    for j in range(G):
                        score_tile(i, p, s, j)
                        if not last:
                            if s == 0 and j == 0:
                                pe.wait_ge(m_in[1 - p], 128 * (use + (1 if p else 0) + 1))
                            max_tile(1 - p, s, j, m_use(i, s, j), m_bank(s, j))
                    if s > 0:
                        pv_step(i, p, s - 1)
                    elif not first:
                        pv_step(i - 1, 1 - p, NS - 1)
                    if s == ROWS2_STEP:
                        max_rows(1, second_rows_use(i, last), second_rows_bank(last),
                                 2 * i + 2)
                    if s == ROWS1_STEP and not last:
                        max_rows(0, rows_use(i, 0), rows_bank(0), 2 * i + 3)

            pe.wait_ge(const_in, 32)
            pe.wait_ge(m_in[0], 128)
            for s in range(NS):
                for j in range(G):
                    use = G * s + j + (s > ROWS1_STEP)
                    max_tile(0, s, j, use, M_BANK + use % NM)
                if s == ROWS1_STEP:
                    use = G * (s + 1)
                    max_rows(0, use, M_BANK + use % NM, 1)
            iteration(0, 0, 0, first=True)
            with pe.Fori(0, NIT // 2 - 1) as u:
                iteration(2 * u + 1, 1, u)
                iteration(2 * u + 2, 0, u + 1)
            iteration(NIT - 1, 1, NIT // 2 - 1, last=True)
            pv_step(NIT - 1, 1, NS - 1)

        @block.vector
        def _(dve):
            def max_of_tile(s, j, use, bank, first=False):
                qt, kc = qtile(s)
                w = min(CH, (qt + 1) * P - kc * CH)
                dve.wait_ge(m_ready, use + 1)
                largest = part[:, qt // 8, j, qt % 8, kc:kc + 1]
                if kc == qt // TPC:
                    if not isinstance(use, int) or use > 0:
                        dve.wait_ge(m_read, use)
                    dve.sem_inc(masking, 1)
                    nc.vector.tensor_tensor_reduce(out=masked[:, j, 0:w], in0=ps[:, bank, 0:w], in1=mask[:, CH - w:CH],
                                                   scale=1.0, scalar=MASKED, op0=ALU.add, op1=ALU.max,
                                                   accum_out=largest).then_inc(m_read, 1)
                else:
                    nc.vector.tensor_reduce(largest, ps[:, bank, 0:w], AX.X, ALU.max).then_inc(m_read, 1)

            def max_of_half(half, read):
                dve.wait_ge(m_read, read)
                nc.vector.tensor_reduce(qmax[:, half, :], part[:, half].rearrange("p j q k -> p (j q) k"), AX.X, ALU.max
                                        ).then_inc(qmax_done, 1)

            def rows_out(i, half, use, bank):
                dve.wait_ge(m_ready, use + 1)
                dve.wait_ge(rows_in[half], 16 * G * i)
                nc.vector.tensor_scalar(nrow[:, half, :], ps[0:G * 8, bank, 0:P], -1.0 / SQK, None, ALU.mult
                                        ).then_inc(m_read, 1)

            def turn(i, c):
                dve.wait_ge(o_copied, NC * i + c + 1)
                nc.vector.transpose(ot[:, c % 2].rearrange("p b r -> p (b r)"), o_sb[:, c % 2]).then_inc(ot_done, 1)
                dve.wait_ge(ot_done, NC * i + c + 1)
                nc.vector.reciprocal(rsum[:, c % 2, :], ot[:, c % 2, :, DK]).then_inc(rsum_done, 1)

            def turn_back(i, c):
                dve.wait_ge(yt_done, NC * i + c + 1)
                nc.vector.transpose(y_sb[:, c % 2], yt[:, c % 2].rearrange("p b r -> p (b r)")).then_inc(y_done, 1)

            def iteration(i, p, first=False, last=False):
                for s in range(NS):
                    if not last:
                        for j in range(G):
                            max_of_tile(s, j, m_use(i, s, j), m_bank(s, j))
                    if s == 0:
                        max_of_half(1, NM + M_BEFORE + i * M_ITER)
                    if s == ROWS2_STEP:
                        rows_out(i, 1, second_rows_use(i, last), second_rows_bank(last))
                        if not first:
                            turn(i - 1, NC - 1)
                    if s == 3 and not first:
                        turn_back(i - 1, NC - 1)
                    if s == HALF_STEP and not last:
                        max_of_half(0, NM + m_use(i, HALF_STEP, 0))
                    if s == ROWS1_STEP and not last:
                        rows_out(i + 1, 0, rows_use(i, 0), rows_bank(0))
                    for c in range(NC - 1):
                        if s == CHUNK_END[c] + 3:
                            turn(i, c)
                        if s == CHUNK_END[c] + 5:
                            turn_back(i, c)

            dve.sem_inc(m_read, NM)
            for p in range(2):
                nc.vector.memset(mq[:, p], 0.0).then_inc(m_preset, 1)
            nc.vector.memset(mk[:], 0.0).then_inc(m_preset, 1)
            nc.vector.memset(part[:], -3e38).then_inc(part_preset, 1)
            dve.wait_ge(const_in, 32)
            dve.wait_ge(part_preset, 1)
            for s in range(NS):
                for j in range(G):
                    use = G * s + j + (s > ROWS1_STEP)
                    max_of_tile(s, j, use, M_BANK + use % NM)
                if s == HALF_STEP:
                    max_of_half(0, NM + G * HALF_STEP)
                if s == ROWS1_STEP:
                    use = G * (s + 1)
                    rows_out(0, 0, use, M_BANK + use % NM)
            iteration(0, 0, first=True)
            with dve.Fori(0, NIT // 2 - 1) as u:
                iteration(2 * u + 1, 1)
                iteration(2 * u + 2, 0)
            iteration(NIT - 1, 1, last=True)
            turn(NIT - 1, NC - 1)
            turn_back(NIT - 1, NC - 1)

        @block.scalar
        def _(act):
            def copy_o(i, c):
                act.wait_ge(pv_done, NS * i + CHUNK_END[c] + 1 + 2)
                act.wait_ge(ylo_done, NC * i + c + 1)
                nc.scalar.copy(o_sb[:, c % 2], ps[:, O_BANK]).then_inc(o_copied, 1)

            def y_split(i, c):
                act.wait_ge(y_done, NC * i + c + 1)
                act.wait_ge(y_out[c % 2], 32 * (2 * i + c // 2))
                nc.scalar.copy(y_hi[:, c % 2], y_sb[:, c % 2]).then_inc(yhi_done, 1)

            def iteration(i, first=False):
                for s in range(NS):
                    c, kb = STEPS[s]
                    q0 = max(0, kb - TPC * c) * P
                    act.wait_ge(pv_done, NS * i + s + 1)
                    for j in range(G):
                        act.wait_ge(s_ready, ST * i + G * s + j + 1)
                        nc.scalar.activation(prob[:, s % 2, j, q0:CH], ps[:, S_BANK + j, q0:CH], ACT.Exp,
                                             scale=1.0 / (SQK * DK ** 0.5)).then_inc(p_done, 1)
                    if s == 0 and not first:
                        copy_o(i - 1, NC - 1)
                    if s == 5 and not first:
                        y_split(i - 1, NC - 1)
                    for cc in range(NC - 1):
                        if s == CHUNK_END[cc] + 1:
                            copy_o(i, cc)
                        if s == CHUNK_END[cc] + 7:
                            y_split(i, cc)

            act.sem_inc(p_done, G)
            iteration(0, first=True)
            with act.Fori(0, NIT // 2 - 1) as u:
                iteration(2 * u + 1)
                iteration(2 * u + 2)
            iteration(NIT - 1)
            copy_o(NIT - 1, NC - 1)
            y_split(NIT - 1, NC - 1)

        @block.gpsimd
        def _(pool):
            nc.gpsimd.memset(aq[:], 0.0).then_inc(a_preset, 1)
            nc.gpsimd.memset(ak[:], SQK).then_inc(a_preset, 1)
            pool.sem_inc(pv_done, 2)
            pool.sem_inc(ylo_done, 2)

            def mask_step(i, s):
                c, kb = STEPS[s]
                q0 = (kb - TPC * c) * P
                block = prob[:, s % 2, :, q0:q0 + P]
                pool.wait_ge(p_done, ST * i + G * s + G + G)
                pool.sem_inc(selecting, 1)
                nc.gpsimd.affine_select(out=block, in_=block, compare_op=ALU.is_ge, fill=0.0, base=0,
                                        pattern=[[0, G], [1, P]], channel_multiplier=-1).then_inc(mask_done, 1)

            def divide(i, c):
                pool.wait_ge(rsum_done, NC * i + c + 1)
                nc.gpsimd.tensor_tensor(yt[:, c % 2], ot[:, c % 2],
                                        rsum[:, c % 2, :].unsqueeze(2).to_broadcast([P, CH // 32, 32]), ALU.mult
                                        ).then_inc(yt_done, 1)

            def y_split(i, c):
                pool.wait_ge(yhi_done, NC * i + c + 1)
                nc.gpsimd.tensor_tensor(y_lo[:, c % 2], y_sb[:, c % 2], y_hi[:, c % 2], ALU.subtract).then_inc(ylo_done, 1)

            def iteration(i, first=False):
                for s in range(NS):
                    if is_diagonal(s):
                        mask_step(i, s)
                    if s == 1 and not first:
                        divide(i - 1, NC - 1)
                    if s == 5 and not first:
                        y_split(i - 1, NC - 1)
                    for c in range(NC - 1):
                        if s == CHUNK_END[c] + 3:
                            divide(i, c)
                        if s == CHUNK_END[c] + 7:
                            y_split(i, c)

            pool.wait_ge(w_in, 16 * len(w_f))
            for q, (f, (hi, lo)) in enumerate(zip(w_f, weights)):
                flat = "p k n -> p (k n)"
                f, hi, lo = f[:].rearrange(flat), hi[:].rearrange(flat), lo[:].rearrange(flat)
                nc.gpsimd.tensor_scalar(f, f, SX, None, ALU.mult).then_inc(w_scaled, 1)
                pool.wait_ge(w_scaled, q + 1)
                nc.gpsimd.tensor_copy(hi, f).then_inc(whi_done, 1)
                pool.wait_ge(whi_done, q + 1)
                nc.gpsimd.tensor_tensor(lo, f, hi, ALU.subtract).then_inc(w_done, 1)
            iteration(0, first=True)
            with pool.Fori(1, NIT) as i:
                iteration(i)
            divide(NIT - 1, NC - 1)
            y_split(NIT - 1, NC - 1)


def stage3(nc, x, att_d, weights, b1, b2, ident_d, out):
    with ExitStack() as ctx:
        def sb(name, shape, dt):
            return ctx.enter_context(nc.sbuf_tensor(name, shape, dt))

        def sem(name):
            return ctx.enter_context(nc.semaphore(name))

        (wo_hi, wo_lo), (w1_hi, w1_lo), (w2_hi, w2_lo) = weights
        ident = sb("s3_ident", [P, P], F32)
        b1_in = sb("s3_b1_in", [P, KF], F32)
        b1_s = sb("s3_b1_s", [P, KF], F32)
        b2_all = sb("s3_b2_all", [P, D], F32)
        eps = sb("s3_eps", [P, 1], F32)
        xin = sb("s3_xin", [P, 2, TPC, D], F32)
        att_hi, att_lo = sb("s3_att_hi", [P, 2, KD, CH], F16), sb("s3_att_lo", [P, 2, KD, CH], F16)
        x2 = sb("s3_x2", [P, 2, TPC, D], F32)
        x2b = sb("s3_x2b", [P, 2, TPC, D], F32)
        xn = sb("s3_xn", [P, 2, TPC, D], F32)
        stats = sb("s3_stats", [P, 2, TPC, 6], F32)
        mv = sb("s3_mv", [P, 2, TPC, 2], F32)
        std = sb("s3_std", [P, 2, TPC], F32)
        rstd = sb("s3_rstd", [P, 2, TPC], F32)
        xt_hi, xt_lo = sb("s3_xt_hi", [P, 2, KD, CH], F16), sb("s3_xt_lo", [P, 2, KD, CH], F16)
        h_f = sb("s3_h_f", [P, 2, CH], F32)
        h_hi, h_lo = sb("s3_h_hi", [P, 2, KF, CH], F16), sb("s3_h_lo", [P, 2, KF, CH], F16)
        y = sb("s3_y", [P, 2, TPC, D], F32)
        ps = ctx.enter_context(nc.psum_tensor("s3_ps", [P, 8, CH], F32))
        A_BANK, XT_BANK, H_BANK, Y_BANK = 0, 2, 4, 6

        w_in, preset, aggregating = sem("s3_w_in"), sem("s3_preset"), sem("s3_aggregating")
        x_in = [sem(f"s3_x_in{p}") for p in range(2)]
        att_in = [sem(f"s3_att_in{p}") for p in range(2)]
        a_ready, x2_done, x2b_done = sem("s3_a_ready"), sem("s3_x2_done"), sem("s3_x2b_done")
        stats_done, mv_done, std_done = sem("s3_stats_done"), sem("s3_mv_done"), sem("s3_std_done")
        rstd_done, xn_done = sem("s3_rstd_done"), sem("s3_xn_done")
        xt_ready, xhi_done, xlo_done = sem("s3_xt_ready"), sem("s3_xhi_done"), sem("s3_xlo_done")
        h_ready, h_done, hhi_done, hlo_done = sem("s3_h_ready"), sem("s3_h_done"), sem("s3_hhi_done"), sem("s3_hlo_done")
        y_ready, y_done = sem("s3_y_ready"), sem("s3_y_done")
        y_out = [sem(f"s3_y_out{p}") for p in range(2)]
        NPAIR = NCHUNK // 2

        block = ctx.enter_context(nc.Block())

        @block.sync
        def _(sp):
            def load_x(n, p):
                sp.dma_start(xin[:, p], x[bass.ds(n * CH, CH), :].rearrange("(t p) d -> p t d", p=P)
                             ).then_inc(x_in[p], 16)

            def load_att(b, cc, p):
                for dst, hl in ((att_hi, 0), (att_lo, 1)):
                    for g in range(NG):
                        src = att_d[hl, bass.ds(NG * b + g, 1), :, cc * CH:(cc + 1) * CH].rearrange(
                            "a (j r) t -> (a j) r t", r=2 * DK)[:, 0:DK, :]
                        sp.dma_start(dst[GC * (g % 2):GC * (g % 2 + 1), p, g // 2, :], src).then_inc(att_in[p], 16)

            def step(b, cc, last):
                n, p = NC * b + cc, cc % 2
                if not (last and cc >= NC - 2):
                    sp.wait_ge(x2_done, 2 * (n + 1) + 2)
                    load_x(n + 2, p)
                    if cc + 2 < NC:
                        load_att(b, cc + 2, p)
                    else:
                        load_att(b + 1, cc + 2 - NC, p)
                for pair in range(2):
                    sp.wait_ge(y_done, 2 * n + pair + 1 + 2)
                    sp.dma_start(out[bass.ds(n * CH + pair * 2 * P, 2 * P), :].rearrange("(t p) d -> p t d", p=P),
                                 y[:, p, 2 * pair:2 * pair + 2]).then_inc(y_out[p], 16)

            load_x(0, 0)
            load_att(0, 0, 0)
            sp.dma_start(ident[:], ident_d).then_inc(w_in, 16)
            sp.dma_start(b1_in[:], b1).then_inc(w_in, 16)
            sp.dma_start(b2_all[:], b2.rearrange("(a d) -> a d", a=1).to_broadcast([P, D])).then_inc(w_in, 16)
            load_x(1, 1)
            load_att(0, 1, 1)
            with sp.Fori(0, B - 1) as b:
                for cc in range(NC):
                    step(b, cc, False)
            for cc in range(NC):
                step(B - 1, cc, True)
            for p in range(2):
                sp.wait_ge(y_out[p], 32 * (NPAIR + 1))

        @block.tensor
        def _(pe):
            def project(n, p, use):
                pe.wait_ge(att_in[p], 16 * 2 * NG * (use + 1))
                for pair in range(2):
                    pe.wait_ge(x2_done, 2 * n + pair + 1)
                    for t in range(2):
                        tt = 2 * pair + t
                        mm = [(a, w, k) for a, w in terms(att_hi, att_lo, wo_hi, wo_lo) for k in range(KD)]
                        for q, (a, w, k) in enumerate(mm):
                            last = nc.tensor.matmul(ps[:, A_BANK + pair, t * D:(t + 1) * D],
                                                    a[:, p, k, tt * P:(tt + 1) * P], w[:, k],
                                                    start=q == 0, stop=q == len(mm) - 1)
                    last.then_inc(a_ready, 1)

            def transposes(n, p):
                pe.wait_ge(xn_done, n + 1)
                pe.wait_ge(xlo_done, n)
                for k in range(KD):
                    for t in range(TPC):
                        last = nc.tensor.transpose(ps[:, XT_BANK + k, t * P:(t + 1) * P],
                                                   xn[:, p, t, k * P:(k + 1) * P], ident[:])
                last.then_inc(xt_ready, 1)

            def ffn1(n, p):
                pe.wait_ge(xlo_done, n + 1)
                for f in range(KF):
                    pe.wait_ge(h_done, KF * n + f + 1)
                    mm = [(w, a, k) for w, a in terms(w1_hi, w1_lo, xt_hi, xt_lo) for k in range(KD)]
                    for q, (w, a, k) in enumerate(mm):
                        last = nc.tensor.matmul(ps[:, H_BANK + f % 2], w[:, k, f * P:(f + 1) * P], a[:, p, k],
                                                start=q == 0, stop=q == len(mm) - 1)
                    last.then_inc(h_ready, 1)

            def ffn2_tile(n, p, tt):
                pair, t = divmod(tt, 2)
                if t == 0:
                    pe.wait_ge(y_done, 2 * n + pair + 1)
                mm = [(a, w, k) for k in range(KF) for a, w in terms(h_hi, h_lo, w2_hi, w2_lo)]
                for q, (a, w, k) in enumerate(mm):
                    last = nc.tensor.matmul(ps[:, Y_BANK + pair, t * D:(t + 1) * D],
                                            a[:, p, k, tt * P:(tt + 1) * P], w[:, k],
                                            start=q == 0, stop=q == len(mm) - 1)
                if t == 1:
                    last.then_inc(y_ready, 1)

            def step(n, p, next_use, last=False):
                ffn1(n, p)
                if not last:
                    project(n + 1, 1 - p, next_use)
                pe.wait_ge(hlo_done, KF * (n + 1) + 2)
                for tt in range(TPC):
                    if tt == TPC - 1 and not last:
                        transposes(n + 1, 1 - p)
                    ffn2_tile(n, p, tt)

            pe.wait_ge(w_in, 48)
            project(0, 0, 0)
            transposes(0, 0)
            with pe.Fori(0, NPAIR - 1) as u:
                step(2 * u, 0, u)
                step(2 * u + 1, 1, u + 1)
            step(NCHUNK - 2, 0, NPAIR - 1)
            step(NCHUNK - 1, 1, 0, last=True)

        @block.vector
        def _(dve):
            def residual(n, p, use):
                dve.wait_ge(x_in[p], 16 * (use + 1))
                for pair in range(2):
                    dve.wait_ge(a_ready, 2 * n + pair + 1)
                    dve.wait_ge(x2b_done, n + 1)
                    nc.vector.scalar_tensor_tensor(x2[:, p, 2 * pair:2 * pair + 2].rearrange("p t d -> p (t d)"),
                                                   ps[:, A_BANK + pair], 1.0 / SQK,
                                                   xin[:, p, 2 * pair:2 * pair + 2].rearrange("p t d -> p (t d)"),
                                                   ALU.mult, ALU.add).then_inc(x2_done, 1)

            def statistics(n, p):
                dve.wait_ge(x2_done, 2 * (n + 1) + 2)
                for t in range(TPC):
                    nc.vector.bn_stats(stats[:, p, t, :], x2[:, p, t, :]).then_inc(stats_done, 1)

            def normalize(n, p):
                dve.wait_ge(stats_done, TPC * (n + 1))
                dve.sem_inc(aggregating, 1)
                for t in range(TPC):
                    last = nc.vector.bn_aggr(mv[:, p, t, :], stats[:, p, t, :])
                last.then_inc(mv_done, 1)
                dve.wait_ge(std_done, n + 1)
                nc.vector.reciprocal(rstd[:, p, :], std[:, p, :]).then_inc(rstd_done, 1)
                dve.wait_ge(rstd_done, n + 1)
                for t in range(TPC):
                    last = nc.vector.tensor_scalar(xn[:, p, t, :], x2[:, p, t, :], mv[:, p, t, 0:1],
                                                   rstd[:, p, t:t + 1], ALU.subtract, ALU.mult)
                last.then_inc(xn_done, 1)

            def split_xt(n, p):
                dve.wait_ge(xhi_done, n + 1)
                for k in range(KD):
                    last = nc.vector.tensor_tensor(xt_lo[:, p, k], ps[:, XT_BANK + k], xt_hi[:, p, k], ALU.subtract)
                last.then_inc(xlo_done, 1)

            def split_h(n, p, f):
                dve.wait_ge(h_done, KF * n + f + 1 + 2)
                nc.vector.tensor_copy(h_hi[:, p, f], h_f[:, f % 2]).then_inc(hhi_done, 1)
                dve.wait_ge(hhi_done, KF * n + f + 1)
                nc.vector.tensor_tensor(h_lo[:, p, f], h_f[:, f % 2], h_hi[:, p, f], ALU.subtract).then_inc(hlo_done, 1)

            def output(n, p, use, pair):
                dve.wait_ge(y_ready, 2 * n + pair + 1)
                dve.wait_ge(x2b_done, n + 1 + 2)
                dve.wait_ge(y_out[p], 32 * (use + 1))
                nc.vector.scalar_tensor_tensor(y[:, p, 2 * pair:2 * pair + 2].rearrange("p t d -> p (t d)"),
                                               ps[:, Y_BANK + pair], 1.0 / (SH * SX),
                                               x2b[:, p, 2 * pair:2 * pair + 2].rearrange("p t d -> p (t d)"),
                                               ALU.mult, ALU.add).then_inc(y_done, 1)

            def step(n, p, use, next_use, last=False):
                for f in range(KF):
                    split_h(n, p, f)
                if not last:
                    residual(n + 1, 1 - p, next_use)
                    statistics(n + 1, 1 - p)
                    normalize(n + 1, 1 - p)
                output(n, p, use, 0)
                if not last:
                    split_xt(n + 1, 1 - p)
                output(n, p, use, 1)

            dve.sem_inc(x2b_done, 2)
            dve.sem_inc(y_done, 2)
            for p in range(2):
                dve.sem_inc(y_out[p], 32)
            dve.sem_inc(x2_done, 2)
            dve.sem_inc(hlo_done, 2)
            nc.vector.memset(eps[:], EPS / SX ** 2).then_inc(preset, 1)
            dve.wait_ge(w_in, 48)
            nc.vector.tensor_scalar(b1_s[:], b1_in[:], SH, None, ALU.mult).then_inc(preset, 1)
            residual(0, 0, 0)
            statistics(0, 0)
            normalize(0, 0)
            split_xt(0, 0)
            with dve.Fori(0, NPAIR - 1) as u:
                step(2 * u, 0, u, u)
                step(2 * u + 1, 1, u, u + 1)
            step(NCHUNK - 2, 0, NPAIR - 1, NPAIR - 1)
            step(NCHUNK - 1, 1, NPAIR - 1, 0, last=True)

        @block.scalar
        def _(act):
            def std_of(n, p):
                act.wait_ge(mv_done, n + 1)
                nc.scalar.activation(std[:, p, :], mv[:, p, :, 1], ACT.Sqrt, bias=eps[:], scale=1.0 / SX ** 2
                                     ).then_inc(std_done, 1)

            def hi_xt(n, p):
                act.wait_ge(xt_ready, n + 1)
                for k in range(KD):
                    last = nc.scalar.copy(xt_hi[:, p, k], ps[:, XT_BANK + k])
                last.then_inc(xhi_done, 1)

            def relu(n, f):
                act.wait_ge(h_ready, KF * n + f + 1)
                act.wait_ge(hlo_done, KF * n + f + 1)
                nc.scalar.activation(h_f[:, f % 2], ps[:, H_BANK + f % 2], ACT.Relu, bias=b1_s[:, f:f + 1],
                                     scale=SH / SQK).then_inc(h_done, 1)

            def step(n, p, last=False):
                for f in range(KF):
                    relu(n, f)
                if not last:
                    std_of(n + 1, 1 - p)
                    hi_xt(n + 1, 1 - p)

            act.sem_inc(h_done, 2)
            act.wait_ge(preset, 2)
            std_of(0, 0)
            hi_xt(0, 0)
            with act.Fori(0, NPAIR - 1) as u:
                step(2 * u, 0)
                step(2 * u + 1, 1)
            step(NCHUNK - 2, 0)
            step(NCHUNK - 1, 1, last=True)

        @block.gpsimd
        def _(pool):
            def add_b2(n, p):
                pool.wait_ge(x2_done, 2 * (n + 1) + 2)
                if not isinstance(n, int) or n > 1:
                    pool.wait_ge(y_done, 2 * n)
                for t in range(TPC):
                    last = nc.gpsimd.tensor_tensor(x2b[:, p, t], x2[:, p, t], b2_all[:], ALU.add)
                last.then_inc(x2b_done, 1)

            pool.wait_ge(w_in, 48)
            add_b2(0, 0)
            add_b2(1, 1)
            with pool.Fori(1, NPAIR) as u:
                add_b2(2 * u, 0)
                add_b2(2 * u + 1, 1)


def layer(nc, x, wqkv, wo, w1, b1, w2, b2, cos_d, sin_d, ident_d, mask_d, out):
    qk_d = nc.dram_tensor("qk_scratch", (NIT, 2, 2, GC, S), F16, kind="Internal").ap()
    v_d = nc.dram_tensor("v_scratch", (P, S // P, NIT, G * 2 * DK), F32, kind="Internal").ap()
    att_d = nc.dram_tensor("att_scratch", (2, NIT, P, S), F16, kind="Internal").ap()
    stage1(nc, x, wqkv, cos_d, sin_d, ident_d, qk_d, v_d)
    with ExitStack() as ctx:
        weights = [[ctx.enter_context(nc.sbuf_tensor(f"{name}_{part}", [P, k, n], F16)) for part in ("hi", "lo")]
                   for name, k, n in (("wo", KD, D), ("w1", KD, F), ("w2", KF, D))]
        stage2(nc, ident_d, mask_d, qk_d, v_d, att_d, (wo, w1, w2), weights)
        stage3(nc, x, att_d, weights, b1, b2, ident_d, out)


def shape_constants():
    freqs = (1.0 / np.float32(10000.0) ** (np.arange(0, DK, 2, dtype=np.float32) / np.float32(DK))).astype(np.float32)
    angles = freqs[(np.arange(P) % DK) // 2][:, None] * np.arange(S, dtype=np.float32)[None, :]
    sign = np.where(np.arange(P) % 2 == 0, -1.0, 1.0)[:, None]
    cos = (np.cos(angles) / SX).astype(np.float32)
    sin = (np.sin(angles) * sign / SX).astype(np.float32)
    r = np.arange(P)
    mask = np.concatenate([np.zeros((P, CH - P)), np.where(r[None, :] > r[:, None], MASKED, 0.0)], axis=1)
    return {"cos": cos, "sin": sin, "ident": np.eye(P, dtype=np.float32), "mask": mask.astype(np.float32)}


def kernel(L0_attn_x, L0_attn_Wq, L0_attn_Wk, L0_attn_Wv, L0_attn_Wo, L0_ffn_w1, L0_ffn_b1, L0_ffn_w2, L0_ffn_b2):
    import concourse.bacc as bacc
    from concourse.bass_utils import run_bass_kernel_spmd

    wq, wk, wv, wo = (np.asarray(w).T for w in (L0_attn_Wq, L0_attn_Wk, L0_attn_Wv, L0_attn_Wo))
    cols = []
    for g in range(NG):
        cols += [wq[:, GC * g:GC * (g + 1)], wk[:, GC * g:GC * (g + 1)]]
    arrays = {
        "x": np.asarray(L0_attn_x).reshape(B * S, D),
        "w_qkv": np.concatenate(cols + [wv], axis=1),
        "w_o": wo,
        "w_1": np.asarray(L0_ffn_w1), "b_1": np.asarray(L0_ffn_b1).reshape(KF, P).T,
        "w_2": np.asarray(L0_ffn_w2), "b_2": np.asarray(L0_ffn_b2),
        **shape_constants(),
    }
    arrays = {name: np.ascontiguousarray(a) for name, a in arrays.items()}
    nc = bacc.Bacc("TRN2", target_bir_lowering=False, num_devices=1)
    args = [nc.dram_tensor(name, a.shape, mybir.dt.from_np(a.dtype), kind="ExternalInput").ap()
            for name, a in arrays.items()]
    out = nc.dram_tensor("out", (B * S, D), F32, kind="ExternalOutput").ap()
    layer(nc, *args, out)
    r = run_bass_kernel_spmd(nc, [arrays], core_ids=[0])
    return r.results[0]["out"].reshape(B, S, D)
```

```python
from contextlib import ExitStack

import numpy as np

import concourse.bass as bass
from concourse import mybir

ALU = mybir.AluOpType
ACT = mybir.ActivationFunctionType
AX = mybir.AxisListType
F32 = mybir.dt.float32
F16 = mybir.dt.float16

P = 128
B, S, D, H, F = 4, 2048, 256, 16, 1024
DK = D // H
CH = 512
NC = S // CH
TPC = CH // P
NCHUNK = B * NC
KD = D // P
KF = F // P
G = 4
NG = H // G
GC = G * DK
NIT = B * NG
EPS = 1e-5

SX = 64.0
SH = 16.0
SQK = SX * SX

ROLE_ROWS = 3 * DK
MAXROW = ROLE_ROWS
HROWS = 64
MROWS = 32 * (G - 1) + DK
AROWS = HROWS + MAXROW + 1

STEPS = [(c, kb) for c in range(NC) for kb in range(TPC * (c + 1))]
NS = len(STEPS)
CHUNK_END = [max(s for s in range(NS) if STEPS[s][0] == c) for c in range(NC)]
HALF_STEP = CHUNK_END[NC // 2 - 1] + 1
UNITS = G * NS
NDIAG = NC * TPC
MASKED = -1e30


def is_diagonal(s):
    c, kb = STEPS[s]
    return kb >= TPC * c


def diagonals(s):
    return sum(is_diagonal(t) for t in range(s))


def terms(a_hi, a_lo, b_hi, b_lo):
    return ((a_hi, b_hi), (a_hi, b_lo), (a_lo, b_hi))


def load_m(sp, ops, qk_d, i, p):
    for j in range(G):
        rows = slice(32 * j, 32 * j + DK)
        for qk, dst in ((0, ops.mq[rows, p, j]), (1, ops.mk[rows, p])):
            src = qk_d[bass.ds(i, 1), qk, 0, DK * j:DK * (j + 1), :].rearrange("a r t -> (a r) t")
            sp.dma_start(dst, src).then_inc(ops.m_in[p], 16)


def load_a(sp, ops, qk_d, i, p):
    for qk, roles in ((0, (0, 1, 0)), (1, (0, 0, 1))):
        for r, hl in enumerate(roles):
            for jj in range(2):
                rows = slice(HROWS * jj + DK * r, HROWS * jj + DK * (r + 1))
                dst = ops.ak[rows, p] if qk else ops.aq[rows, p, jj:G:2]
                src = qk_d[bass.ds(i, 1), qk, hl].rearrange("a (jp jj r) t -> (a jj) r jp t", jj=2, r=DK)
                sp.dma_start(dst, src[jj]).then_inc(ops.a_in[p], 16)


class Operands:
    def __init__(self, nc, ctx):
        self.mq = ctx.enter_context(nc.sbuf_tensor("mq", [P, 2, G, S], F16))
        self.mk = ctx.enter_context(nc.sbuf_tensor("mk", [P, 2, S], F16))
        self.aq = ctx.enter_context(nc.sbuf_tensor("aq", [P, 2, G, S], F16))
        self.ak = ctx.enter_context(nc.sbuf_tensor("ak", [P, 2, G // 2, S], F16))
        self.m_in = [ctx.enter_context(nc.semaphore(f"m_in{p}")) for p in range(2)]
        self.a_in = [ctx.enter_context(nc.semaphore(f"a_in{p}")) for p in range(2)]


def stage1(nc, x, w_qkv, cos_d, sin_d, ident_d, qk_d, v_d, ops):
    with ExitStack() as ctx:
        def sb(name, shape, dt):
            return ctx.enter_context(nc.sbuf_tensor(name, shape, dt))

        def sem(name):
            return ctx.enter_context(nc.semaphore(name))

        NW = 3 * D
        w_f = sb("s1_w_f", [P, KD, NW], F32)
        w_hi = sb("s1_w_hi", [P, KD, NW], F16)
        w_lo = sb("s1_w_lo", [P, KD, NW], F16)
        cos = sb("s1_cos", [P, S], F32)
        sin = sb("s1_sin", [P, S], F32)
        ident = sb("s1_ident", [P, P], F32)
        eps = sb("s1_eps", [P, 1], F32)
        xin = sb("s1_xin", [P, 2, TPC, D], F32)
        xn = sb("s1_xn", [P, 2, TPC, D], F32)
        stats = sb("s1_stats", [P, 2, TPC, 6], F32)
        mv = sb("s1_mv", [P, 2, TPC, 2], F32)
        negmean = sb("s1_negmean", [P, 2, TPC], F32)
        std = sb("s1_std", [P, 2, TPC], F32)
        rstd = sb("s1_rstd", [P, 2, TPC], F32)
        xt_hi = sb("s1_xt_hi", [P, 2, KD, CH], F16)
        xt_lo = sb("s1_xt_lo", [P, 2, KD, CH], F16)
        rot_a = sb("s1_rot_a", [P, NG, CH], F32)
        rot_b = sb("s1_rot_b", [P, NG, CH], F32)
        r_hi = sb("s1_r_hi", [P, NG, CH], F16)
        r_lo = sb("s1_r_lo", [P, NG, CH], F16)
        vst = sb("s1_vst", [P, 2, 2, H, 2 * DK], F32)
        ps = ctx.enter_context(nc.psum_tensor("s1_ps", [P, 8, CH], F32))
        XT_BANK, QK_BANK, V_BANK = 0, 2, 6

        ident_in, w_in, trig_in = sem("s1_ident_in"), sem("s1_w_in"), sem("s1_trig_in")
        whi_done, w_done = sem("s1_whi_done"), sem("s1_w_done")
        eps_preset, v_preset, ops_preset = sem("s1_eps_preset"), sem("s1_v_preset"), sem("s1_ops_preset")
        x_in = [sem(f"s1_x_in{p}") for p in range(2)]
        stats_done, mv_done, std_done = sem("s1_stats_done"), sem("s1_mv_done"), sem("s1_std_done")
        aggregating, mean_done = sem("s1_aggregating"), sem("s1_mean_done")
        rstd_done, centred, xn_done = sem("s1_rstd_done"), sem("s1_centred"), sem("s1_xn_done")
        xt_ready, xhi_done, xlo_done = sem("s1_xt_ready"), sem("s1_xhi_done"), sem("s1_xlo_done")
        qk_ready, v_ready = sem("s1_qk_ready"), sem("s1_v_ready")
        rot_read, rotsin_done, rot_done = sem("s1_rot_read"), sem("s1_rotsin_done"), sem("s1_rot_done")
        rhi_done, rlo_done = sem("s1_rhi_done"), sem("s1_rlo_done")
        v_copied = sem("s1_v_copied")
        qk_out = [sem(f"s1_qk_out{g}") for g in range(NG)]
        v_out = [sem(f"s1_v_out{pair}") for pair in range(2)]

        block = ctx.enter_context(nc.Block())

        def steps(step, engine):
            for cc in range(NC):
                step(cc, cc, 0, cc == 0, NC)
            with engine.Fori(1, B - 1) as b:
                for cc in range(NC):
                    step(NC * b + cc, cc, b, False, NC)
            for cc in range(NC):
                step(NCHUNK - NC + cc, cc, B - 1, False, NC - cc)

        @block.sync
        def _(sp):
            def load_x(n, p):
                sp.dma_start(xin[:, p], x[bass.ds(n * CH, CH), :].rearrange("(t p) d -> p t d", p=P)
                             ).then_inc(x_in[p], 16)

            for g in range(NG):
                sp.sem_inc(qk_out[g], 32)
            for pair in range(2):
                sp.sem_inc(v_out[pair], 16)
            load_x(0, 0)
            sp.dma_start(ident[:], ident_d).then_inc(ident_in, 16)
            sp.dma_start(w_f[:], w_qkv.rearrange("(k p) n -> p k n", p=P)).then_inc(w_in, 16)
            load_x(1, 1)
            for dst, src in ((cos, cos_d), (sin, sin_d)):
                sp.dma_start(dst[:], src).then_inc(trig_in, 16)
            sp.wait_ge(xn_done, 1)
            load_x(2, 0)

            def step(n, cc, b, first, left):
                for g in range(NG):
                    sp.wait_ge(rlo_done, NG * (n + 1) + g + 1)
                    for hl, src in ((1, r_lo), (0, r_hi)):
                        dst = qk_d[bass.ds(NG * b + g, 1), :, hl, :, cc * CH:(cc + 1) * CH].rearrange(
                            "a q r t -> (a q) r t")
                        sp.dma_start(dst, src[:, g, :]).then_inc(qk_out[g], 16)
                    if g == 0 and left > 3:
                        sp.wait_ge(xn_done, n + 2)
                        load_x(n + 3, (cc + 1) % 2)
                for pair in range(2):
                    sp.wait_ge(v_copied, 2 * (n + 1) + pair + 1)
                    dst = v_d[:, TPC * cc + 2 * pair:TPC * cc + 2 * pair + 2, bass.ds(NG * b, NG), :].rearrange(
                        "p t g n -> p t (g n)")
                    sp.dma_start(dst, vst[:, pair].rearrange("p t h e -> p t (h e)")).then_inc(v_out[pair], 16)
                if left == 3:
                    sp.wait_ge(ops_preset, 4)
                    for i in range(2):
                        sp.wait_ge(qk_out[i], 32 * (NC + 1))
                        load_m(sp, ops, qk_d, i, i)
                if left == 2:
                    load_a(sp, ops, qk_d, 0, 0)

            steps(step, sp)
            for g in range(NG):
                sp.wait_ge(qk_out[g], 32 * (NCHUNK + 1))
            for pair in range(2):
                sp.wait_ge(v_out[pair], 16 * (NCHUNK + 1))

        @block.tensor
        def _(pe):
            def transposes(n, p):
                pe.wait_ge(xn_done, n + 1)
                if not isinstance(n, int) or n > 0:
                    pe.wait_ge(xlo_done, n)
                for k in range(KD):
                    for t in range(TPC):
                        last = nc.tensor.transpose(ps[:, XT_BANK + k, t * P:(t + 1) * P],
                                                   xn[:, p, t, k * P:(k + 1) * P], ident[:])
                last.then_inc(xt_ready, 1)

            def project_qk(n, p, g):
                pe.wait_ge(rot_read, NG * n + g + 1)
                mm = [(w, xt, k) for w, xt in terms(w_hi, w_lo, xt_hi, xt_lo) for k in range(KD)]
                for q, (w, xt, k) in enumerate(mm):
                    last = nc.tensor.matmul(ps[:, QK_BANK + g], w[:, k, 2 * GC * g:2 * GC * (g + 1)], xt[:, p, k],
                                            start=q == 0, stop=q == len(mm) - 1)
                last.then_inc(qk_ready, 1)

            def project_v(n, p):
                for pair in range(2):
                    pe.wait_ge(v_copied, 2 * n + pair + 1)
                    for t in range(2):
                        mm = [(xt, w, k) for xt, w in terms(xt_hi, xt_lo, w_hi, w_lo) for k in range(KD)]
                        for q, (xt, w, k) in enumerate(mm):
                            tt = 2 * pair + t
                            last = nc.tensor.matmul(ps[:, V_BANK + pair, t * D:(t + 1) * D],
                                                    xt[:, p, k, tt * P:(tt + 1) * P], w[:, k, 2 * D:3 * D],
                                                    start=q == 0, stop=q == len(mm) - 1)
                    last.then_inc(v_ready, 1)

            def step(n, cc, b, first, left):
                p = cc % 2
                pe.wait_ge(xlo_done, n + 1)
                project_qk(n, p, 0)
                project_qk(n, p, 1)
                if left > 1:
                    transposes(n + 1, 1 - p)
                project_qk(n, p, 2)
                project_qk(n, p, 3)
                project_v(n, p)

            pe.wait_ge(ident_in, 16)
            transposes(0, 0)
            pe.wait_ge(w_done, 1)
            steps(step, pe)

        @block.vector
        def _(dve):
            def statistics(n, p, use):
                dve.wait_ge(x_in[p], 16 * (use + 1))
                for t in range(TPC):
                    nc.vector.bn_stats(stats[:, p, t, :], xin[:, p, t, :]).then_inc(stats_done, 1)

            def aggregate(n, p):
                dve.wait_ge(stats_done, TPC * (n + 1))
                dve.sem_inc(aggregating, 1)
                for t in range(TPC):
                    last = nc.vector.bn_aggr(mv[:, p, t, :], stats[:, p, t, :])
                last.then_inc(mv_done, 1)
                dve.wait_ge(mv_done, n + 1)
                nc.vector.tensor_scalar(negmean[:, p, :], mv[:, p, :, 0], -1.0, None, ALU.mult).then_inc(mean_done, 1)

            def invert_std(n, p):
                dve.wait_ge(std_done, n + 1)
                nc.vector.reciprocal(rstd[:, p, :], std[:, p, :]).then_inc(rstd_done, 1)

            def split_xt(n, p):
                dve.wait_ge(xhi_done, n + 1)
                for k in range(KD):
                    last = nc.vector.tensor_tensor(xt_lo[:, p, k], ps[:, XT_BANK + k], xt_hi[:, p, k], ALU.subtract)
                last.then_inc(xlo_done, 1)

            def rope(n, cc, g):
                tok = slice(cc * CH, (cc + 1) * CH)
                dve.wait_ge(qk_ready, NG * n + g + 1)
                dve.wait_ge(rlo_done, NG * n + g + 1)
                nc.vector.tensor_tensor(rot_a[:, g], ps[:, QK_BANK + g], cos[:, tok], ALU.mult)
                nc.vector.stream_shuffle(rot_b[:, g], ps[:, QK_BANK + g], [r ^ 1 for r in range(32)]
                                         ).then_inc(rot_read, 1)

            def split_rot(n, g):
                dve.wait_ge(rhi_done, NG * n + g + 1)
                nc.vector.tensor_tensor(r_lo[:, g], rot_a[:, g], r_hi[:, g], ALU.subtract).then_inc(rlo_done, 1)

            def step(n, cc, b, first, left):
                p = cc % 2
                rope(n, cc, 0)
                if not first:
                    split_rot(n - 1, 2)
                rope(n, cc, 1)
                if not first:
                    split_rot(n - 1, 3)
                if left > 2:
                    statistics(n + 2, p, 2 * b + cc // 2 + 1)
                    aggregate(n + 2, p)
                rope(n, cc, 2)
                if left > 2:
                    invert_std(n + 2, p)
                if left > 1:
                    split_xt(n + 1, 1 - p)
                rope(n, cc, 3)
                split_rot(n, 0)
                split_rot(n, 1)

            dve.sem_inc(rot_read, NG)
            dve.sem_inc(rlo_done, NG)
            nc.vector.memset(eps[:], EPS / SX ** 2).then_inc(eps_preset, 1)
            for n in range(2):
                statistics(n, n, 0)
                aggregate(n, n)
                invert_std(n, n)
            split_xt(0, 0)
            dve.wait_ge(whi_done, 1)
            nc.vector.scalar_tensor_tensor(w_lo[:].rearrange("p k n -> p (k n)"), w_f[:].rearrange("p k n -> p (k n)"),
                                           SX, w_hi[:].rearrange("p k n -> p (k n)"), ALU.mult, ALU.subtract
                                           ).then_inc(w_done, 1)
            nc.vector.memset(ops.ak[:], SQK).then_inc(ops_preset, 1)
            dve.wait_ge(trig_in, 32)
            steps(step, dve)
            for g in (2, 3):
                split_rot(NCHUNK - 1, g)

        @block.gpsimd
        def _(pool):
            nc.gpsimd.memset(vst[:], 1.0 / SX).then_inc(v_preset, 1)
            for buffer in (ops.mq, ops.mk, ops.aq):
                nc.gpsimd.memset(buffer[:].bitcast(F32), 0.0).then_inc(ops_preset, 1)
            pool.wait_ge(trig_in, 32)
            with pool.Fori(0, B) as b:
                for cc in range(NC):
                    for g in range(NG):
                        u = NG * (NC * b + cc) + g
                        tok = slice(cc * CH, (cc + 1) * CH)
                        pool.wait_ge(rot_read, u + 1 + NG)
                        nc.gpsimd.tensor_tensor(rot_b[:, g], rot_b[:, g], sin[:, tok], ALU.mult).then_inc(rotsin_done, 1)
                        pool.wait_ge(rotsin_done, u + 1)
                        nc.gpsimd.tensor_tensor(rot_a[:, g], rot_a[:, g], rot_b[:, g], ALU.add).then_inc(rot_done, 1)

        @block.scalar
        def _(act):
            def std_of(n, p):
                act.wait_ge(mv_done, n + 1)
                nc.scalar.activation(std[:, p, :], mv[:, p, :, 1], ACT.Sqrt, bias=eps[:], scale=1.0 / SX ** 2
                                     ).then_inc(std_done, 1)

            def centre(n, p):
                act.wait_ge(mean_done, n + 1)
                if not isinstance(n, int) or n > 1:
                    act.wait_ge(xt_ready, n - 1)
                for t in range(TPC):
                    last = nc.scalar.activation(xn[:, p, t, :], xin[:, p, t, :], ACT.Identity, bias=negmean[:, p, t:t + 1])
                last.then_inc(centred, 1)

            def scale_rows(n, p):
                act.wait_ge(rstd_done, n + 1)
                act.wait_ge(centred, n + 1)
                for t in range(TPC):
                    last = nc.scalar.activation(xn[:, p, t, :], xn[:, p, t, :], ACT.Copy, scale=rstd[:, p, t:t + 1])
                last.then_inc(xn_done, 1)

            def hi_xt(n, p):
                act.wait_ge(xt_ready, n + 1)
                for k in range(KD):
                    last = nc.scalar.copy(xt_hi[:, p, k], ps[:, XT_BANK + k])
                last.then_inc(xhi_done, 1)

            def hi_rot(n, g):
                act.wait_ge(rot_done, NG * n + g + 1)
                act.wait_ge(qk_out[g], 32 * (n + 1))
                nc.scalar.copy(r_hi[:, g], rot_a[:, g]).then_inc(rhi_done, 1)

            def stage_v(n, pair):
                act.wait_ge(v_ready, 2 * n + pair + 1)
                act.wait_ge(v_out[pair], 16 * (n + 1))
                nc.scalar.activation(vst[:, pair, :, :, 0:DK],
                                     ps[:, V_BANK + pair].rearrange("p (t h e) -> p t h e", t=2, e=DK),
                                     ACT.Copy, scale=1.0 / SQK).then_inc(v_copied, 1)

            def step(n, cc, b, first, left):
                p = cc % 2
                if not first:
                    hi_rot(n - 1, 2)
                    stage_v(n - 1, 0)
                    hi_rot(n - 1, 3)
                    stage_v(n - 1, 1)
                if left > 1:
                    hi_xt(n + 1, 1 - p)
                if left > 2:
                    std_of(n + 2, p)
                    centre(n + 2, p)
                hi_rot(n, 0)
                if left > 2:
                    scale_rows(n + 2, p)
                hi_rot(n, 1)

            act.sem_inc(v_copied, 2)
            act.wait_ge(eps_preset, 1)
            for n in range(2):
                std_of(n, n)
                centre(n, n)
                scale_rows(n, n)
                if n == 0:
                    hi_xt(0, 0)
                    act.wait_ge(w_in, 16)
                    nc.scalar.activation(w_hi[:], w_f[:], ACT.Copy, scale=SX).then_inc(whi_done, 1)
            act.wait_ge(v_preset, 1)
            steps(step, act)
            hi_rot(NCHUNK - 1, 2)
            stage_v(NCHUNK - 1, 0)
            hi_rot(NCHUNK - 1, 3)
            stage_v(NCHUNK - 1, 1)


def stage2(nc, ident_d, mask_d, qk_d, v_d, att_d, weight_ds, weights, ops):
    with ExitStack() as ctx:
        def sb(name, shape, dt):
            return ctx.enter_context(nc.sbuf_tensor(name, shape, dt))

        def sem(name):
            return ctx.enter_context(nc.semaphore(name))

        ident = sb("s2_ident", [P, P], F32)
        mask = sb("s2_mask", [P, CH], F32)
        masked = sb("s2_masked", [P, G, CH], F32)
        mq, mk, aq, ak, m_in, a_in = ops.mq, ops.mk, ops.aq, ops.ak, ops.m_in, ops.a_in
        v = sb("s2_v", [P, 2, S // P, G, 2 * DK], F32)
        part = sb("s2_part", [P, 2, G, 8, NC], F32)
        qmax = sb("s2_qmax", [P, 2, G * 8], F32)
        nrow = sb("s2_nrow", [G * 8, 2, P], F16)
        prob = sb("s2_prob", [P, 2, G, CH], F32)
        o_sb = sb("s2_o", [P, 2, CH], F32)
        ot = sb("s2_ot", [P, 2, CH // 32, 32], F32)
        rsum = sb("s2_rsum", [P, 2, CH // 32], F32)
        yt = sb("s2_yt", [P, 2, CH // 32, 32], F32)
        y_sb = sb("s2_y", [P, 2, CH], F32)
        y_hi = sb("s2_y_hi", [P, 2, CH], F16)
        y_lo = sb("s2_y_lo", [P, 2, CH], F16)
        w_f = [sb(f"s2_w{q}_f", hi.shape, F32) for q, (hi, lo) in enumerate(weights)]
        ps = ctx.enter_context(nc.psum_tensor("s2_ps", [P, 8, CH], F32))
        M_BANK, NM, S_BANK, O_BANK = 0, 3, 3, 7
        A_DMAS = 2 * 3 * 2

        const_in = sem("s2_const_in")
        part_preset = sem("s2_part_preset")
        v_in = [sem(f"s2_v_in{p}") for p in range(2)]
        m_ready, m_read = sem("s2_m_ready"), sem("s2_m_read")
        qmax_done = sem("s2_qmax_done")
        w_in, w_scaled, whi_done, w_done = sem("s2_w_in"), sem("s2_w_scaled"), sem("s2_whi_done"), sem("s2_w_done")
        masking, selecting = sem("s2_masking"), sem("s2_selecting")
        rows_in = [sem(f"s2_rows_in{h}") for h in range(2)]
        s_ready, p_done, mask_done = sem("s2_s_ready"), sem("s2_p_done"), sem("s2_mask_done")
        pv_done, o_copied = sem("s2_pv_done"), sem("s2_o_copied")
        ot_done, rsum_done, yt_done = sem("s2_ot_done"), sem("s2_rsum_done"), sem("s2_yt_done")
        y_done, yhi_done, ylo_done = sem("s2_y_done"), sem("s2_yhi_done"), sem("s2_ylo_done")
        y_out = [sem(f"s2_y_out{p}") for p in range(2)]

        M_BEFORE, M_ITER = UNITS + 1, UNITS + 2
        ROWS2_STEP, ROWS1_STEP = 1, HALF_STEP + 1
        ST = G * NS

        def m_use(i, s, j):
            return M_BEFORE + i * M_ITER + G * s + j + (s > ROWS2_STEP) + (s > ROWS1_STEP)

        def rows_use(i, half):
            s = (ROWS1_STEP, ROWS2_STEP)[half]
            return M_BEFORE + i * M_ITER + G * (s + 1) + (half == 0)

        def bank_of(local):
            return M_BANK + (M_BEFORE + local) % NM

        assert M_ITER % NM == 0
        def m_bank(s, j):
            return bank_of(G * s + j + (s > ROWS2_STEP) + (s > ROWS1_STEP))

        def rows_bank(half):
            s = (ROWS1_STEP, ROWS2_STEP)[half]
            return bank_of(G * (s + 1) + (half == 0))

        def second_rows_use(i, last):
            return M_BEFORE + i * M_ITER if last else rows_use(i, 1)

        def second_rows_bank(last):
            return bank_of(0) if last else rows_bank(1)

        def qtile(s):
            c, kb = STEPS[s]
            return TPC * c + kb // (c + 1), kb % (c + 1)

        block = ctx.enter_context(nc.Block())

        @block.sync
        def _(sp):
            def load_v(i, p):
                sp.dma_start(v[:, p].rearrange("p k j e -> p k (j e)"),
                             v_d[:, :, bass.ds(i, 1), :].rearrange("p k a n -> p k (a n)")).then_inc(v_in[p], 16)

            def rows(i, p, half, use):
                sp.wait_ge(m_read, NM + use + 1)
                for j in range(G):
                    row = HROWS * (j % 2) + MAXROW
                    sp.dma_start(aq[row:row + 1, p, j, half * S // 2:(half + 1) * S // 2],
                                 nrow[8 * j:8 * j + 8, half, :]).then_inc(rows_in[half], 16)

            def store(i, c):
                sp.wait_ge(ylo_done, NC * i + c + 1 + 2)
                for hl, src in ((1, y_lo), (0, y_hi)):
                    dst = att_d[hl, bass.ds(i, 1), :, c * CH:(c + 1) * CH].rearrange("a p t -> (a p) t")
                    sp.dma_start(dst, src[:, c % 2]).then_inc(y_out[c % 2], 16)

            def iteration(i, p, first=False, last=False, load2=True):
                if load2:
                    sp.wait_ge(m_ready, M_BEFORE + i * M_ITER)
                    load_m(sp, ops, qk_d, i + 2, p)
                rows(i, p, 1, second_rows_use(i, last))
                if not first:
                    store(i - 1, NC - 1)
                if not last:
                    if not first:
                        sp.wait_ge(pv_done, NS * i + 2)
                    load_a(sp, ops, qk_d, i + 1, 1 - p)
                    load_v(i + 1, 1 - p)
                store(i, 0)
                if not last:
                    rows(i + 1, 1 - p, 0, rows_use(i, 0))
                store(i, 1)
                store(i, 2)

            sp.dma_start(ident[:], ident_d).then_inc(const_in, 16)
            sp.dma_start(mask[:], mask_d).then_inc(const_in, 16)
            load_v(0, 0)
            for dst, src in zip(w_f, weight_ds):
                sp.dma_start(dst[:], src.rearrange("(k p) n -> p k n", p=P)).then_inc(w_in, 16)
            rows(0, 0, 0, M_BEFORE - 1)
            iteration(0, 0, first=True)
            with sp.Fori(1, NIT - 3, 2) as i:
                iteration(i, 1)
                iteration(i + 1, 0)
            iteration(NIT - 3, 1)
            iteration(NIT - 2, 0, load2=False)
            iteration(NIT - 1, 1, last=True, load2=False)
            store(NIT - 1, NC - 1)
            for p in range(2):
                sp.wait_ge(y_out[p], 16 * 2 * NIT * NC // 2)

        @block.tensor
        def _(pe):
            def max_tile(p, s, j, use, bank):
                qt, kc = qtile(s)
                w = min(CH, (qt + 1) * P - kc * CH)
                pe.wait_ge(m_read, use + 1)
                nc.tensor.matmul(ps[:, bank, 0:w], mq[0:MROWS, p, j, qt * P:(qt + 1) * P],
                                 mk[0:MROWS, p, kc * CH:kc * CH + w], start=True, stop=True).then_inc(m_ready, 1)

            def max_rows(half, use, bank, qmax_count):
                pe.wait_ge(qmax_done, qmax_count)
                pe.wait_ge(m_read, use + 1)
                nc.tensor.transpose(ps[0:G * 8, bank, 0:P], qmax[:, half, :], ident[:]).then_inc(m_ready, 1)

            def score_tile(i, p, s, j):
                c, kb = STEPS[s]
                q0 = max(0, kb - TPC * c) * P
                pe.wait_ge(p_done, ST * i + G * s + j + 1)
                nc.tensor.matmul(ps[:, S_BANK + j, q0:CH], ak[0:AROWS, p, j // 2, kb * P:(kb + 1) * P],
                                 aq[0:AROWS, p, j, c * CH + q0:(c + 1) * CH], start=True, stop=True
                                 ).then_inc(s_ready, 1)

            def pv_step(i, p, s):
                c, kb = STEPS[s]
                q0 = max(0, kb - TPC * c) * P
                if kb == 0:
                    pe.wait_ge(o_copied, NC * i + c)
                if is_diagonal(s):
                    pe.wait_ge(mask_done, NDIAG * i + diagonals(s) + 1)
                else:
                    pe.wait_ge(p_done, ST * i + G * s + G + G)
                for j in range(G):
                    last = nc.tensor.matmul(ps[32 * j:32 * j + 32, O_BANK, q0:CH], v[:, p, kb, j, :],
                                            prob[:, s % 2, j, q0:CH], start=kb == 0, stop=kb == TPC * (c + 1) - 1)
                last.then_inc(pv_done, 1)

            def iteration(i, p, use, first=False, last=False):
                pe.wait_ge(a_in[p], A_DMAS * 16 * (use + 1))
                pe.wait_ge(v_in[p], 16 * (use + 1))
                pe.wait_ge(rows_in[0], 16 * G * (i + 1))
                for s in range(NS):
                    if s == HALF_STEP:
                        pe.wait_ge(rows_in[1], 16 * G * (i + 1))
                    for j in range(G):
                        score_tile(i, p, s, j)
                        if not last:
                            if s == 0 and j == 0:
                                pe.wait_ge(m_in[1 - p], 128 * (use + (1 if p else 0) + 1))
                            max_tile(1 - p, s, j, m_use(i, s, j), m_bank(s, j))
                    if s > 0:
                        pv_step(i, p, s - 1)
                    elif not first:
                        pv_step(i - 1, 1 - p, NS - 1)
                    if s == ROWS2_STEP:
                        max_rows(1, second_rows_use(i, last), second_rows_bank(last),
                                 2 * i + 2)
                    if s == ROWS1_STEP and not last:
                        max_rows(0, rows_use(i, 0), rows_bank(0), 2 * i + 3)

            pe.wait_ge(const_in, 32)
            pe.wait_ge(m_in[0], 128)
            for s in range(NS):
                for j in range(G):
                    use = G * s + j + (s > ROWS1_STEP)
                    max_tile(0, s, j, use, M_BANK + use % NM)
                if s == ROWS1_STEP:
                    use = G * (s + 1)
                    max_rows(0, use, M_BANK + use % NM, 1)
            iteration(0, 0, 0, first=True)
            with pe.Fori(0, NIT // 2 - 1) as u:
                iteration(2 * u + 1, 1, u)
                iteration(2 * u + 2, 0, u + 1)
            iteration(NIT - 1, 1, NIT // 2 - 1, last=True)
            pv_step(NIT - 1, 1, NS - 1)

        @block.vector
        def _(dve):
            def max_of_tile(s, j, use, bank, first=False):
                qt, kc = qtile(s)
                w = min(CH, (qt + 1) * P - kc * CH)
                dve.wait_ge(m_ready, use + 1)
                largest = part[:, qt // 8, j, qt % 8, kc:kc + 1]
                if kc == qt // TPC:
                    if not isinstance(use, int) or use > 0:
                        dve.wait_ge(m_read, use)
                    dve.sem_inc(masking, 1)
                    nc.vector.tensor_tensor_reduce(out=masked[:, j, 0:w], in0=ps[:, bank, 0:w], in1=mask[:, CH - w:CH],
                                                   scale=1.0, scalar=MASKED, op0=ALU.add, op1=ALU.max,
                                                   accum_out=largest).then_inc(m_read, 1)
                else:
                    nc.vector.tensor_reduce(largest, ps[:, bank, 0:w], AX.X, ALU.max).then_inc(m_read, 1)

            def max_of_half(half, read):
                dve.wait_ge(m_read, read)
                nc.vector.tensor_reduce(qmax[:, half, :], part[:, half].rearrange("p j q k -> p (j q) k"), AX.X, ALU.max
                                        ).then_inc(qmax_done, 1)

            def rows_out(i, half, use, bank):
                dve.wait_ge(m_ready, use + 1)
                dve.wait_ge(rows_in[half], 16 * G * i)
                nc.vector.tensor_scalar(nrow[:, half, :], ps[0:G * 8, bank, 0:P], -1.0 / SQK, None, ALU.mult
                                        ).then_inc(m_read, 1)

            def turn(i, c):
                dve.wait_ge(o_copied, NC * i + c + 1)
                nc.vector.transpose(ot[:, c % 2].rearrange("p b r -> p (b r)"), o_sb[:, c % 2]).then_inc(ot_done, 1)
                dve.wait_ge(ot_done, NC * i + c + 1)
                nc.vector.reciprocal(rsum[:, c % 2, :], ot[:, c % 2, :, DK]).then_inc(rsum_done, 1)

            def turn_back(i, c):
                dve.wait_ge(yt_done, NC * i + c + 1)
                nc.vector.transpose(y_sb[:, c % 2], yt[:, c % 2].rearrange("p b r -> p (b r)")).then_inc(y_done, 1)

            def iteration(i, p, first=False, last=False):
                for s in range(NS):
                    if not last:
                        for j in range(G):
                            max_of_tile(s, j, m_use(i, s, j), m_bank(s, j))
                    if s == 0:
                        max_of_half(1, NM + M_BEFORE + i * M_ITER)
                    if s == ROWS2_STEP:
                        rows_out(i, 1, second_rows_use(i, last), second_rows_bank(last))
                        if not first:
                            turn(i - 1, NC - 1)
                    if s == 3 and not first:
                        turn_back(i - 1, NC - 1)
                    if s == HALF_STEP and not last:
                        max_of_half(0, NM + m_use(i, HALF_STEP, 0))
                    if s == ROWS1_STEP and not last:
                        rows_out(i + 1, 0, rows_use(i, 0), rows_bank(0))
                    for c in range(NC - 1):
                        if s == CHUNK_END[c] + 3:
                            turn(i, c)
                        if s == CHUNK_END[c] + 5:
                            turn_back(i, c)

            dve.sem_inc(m_read, NM)
            nc.vector.memset(part[:], -3e38).then_inc(part_preset, 1)
            dve.wait_ge(const_in, 32)
            dve.wait_ge(part_preset, 1)
            for s in range(NS):
                for j in range(G):
                    use = G * s + j + (s > ROWS1_STEP)
                    max_of_tile(s, j, use, M_BANK + use % NM)
                if s == HALF_STEP:
                    max_of_half(0, NM + G * HALF_STEP)
                if s == ROWS1_STEP:
                    use = G * (s + 1)
                    rows_out(0, 0, use, M_BANK + use % NM)
            iteration(0, 0, first=True)
            with dve.Fori(0, NIT // 2 - 1) as u:
                iteration(2 * u + 1, 1)
                iteration(2 * u + 2, 0)
            iteration(NIT - 1, 1, last=True)
            turn(NIT - 1, NC - 1)
            turn_back(NIT - 1, NC - 1)

        @block.scalar
        def _(act):
            def copy_o(i, c):
                act.wait_ge(pv_done, NS * i + CHUNK_END[c] + 1 + 2)
                act.wait_ge(ylo_done, NC * i + c + 1)
                nc.scalar.copy(o_sb[:, c % 2], ps[:, O_BANK]).then_inc(o_copied, 1)

            def y_split(i, c):
                act.wait_ge(y_done, NC * i + c + 1)
                act.wait_ge(y_out[c % 2], 32 * (2 * i + c // 2))
                nc.scalar.copy(y_hi[:, c % 2], y_sb[:, c % 2]).then_inc(yhi_done, 1)

            def iteration(i, first=False):
                for s in range(NS):
                    c, kb = STEPS[s]
                    q0 = max(0, kb - TPC * c) * P
                    act.wait_ge(pv_done, NS * i + s + 1)
                    for j in range(G):
                        act.wait_ge(s_ready, ST * i + G * s + j + 1)
                        nc.scalar.activation(prob[:, s % 2, j, q0:CH], ps[:, S_BANK + j, q0:CH], ACT.Exp,
                                             scale=1.0 / (SQK * DK ** 0.5)).then_inc(p_done, 1)
                    if s == 0 and not first:
                        copy_o(i - 1, NC - 1)
                    if s == 5 and not first:
                        y_split(i - 1, NC - 1)
                    for cc in range(NC - 1):
                        if s == CHUNK_END[cc] + 1:
                            copy_o(i, cc)
                        if s == CHUNK_END[cc] + 7:
                            y_split(i, cc)

            act.sem_inc(p_done, G)
            iteration(0, first=True)
            with act.Fori(0, NIT // 2 - 1) as u:
                iteration(2 * u + 1)
                iteration(2 * u + 2)
            iteration(NIT - 1)
            copy_o(NIT - 1, NC - 1)
            y_split(NIT - 1, NC - 1)

        @block.gpsimd
        def _(pool):
            pool.sem_inc(pv_done, 2)
            pool.sem_inc(ylo_done, 2)

            def mask_step(i, s):
                c, kb = STEPS[s]
                q0 = (kb - TPC * c) * P
                block = prob[:, s % 2, :, q0:q0 + P]
                pool.wait_ge(p_done, ST * i + G * s + G + G)
                pool.sem_inc(selecting, 1)
                nc.gpsimd.affine_select(out=block, in_=block, compare_op=ALU.is_ge, fill=0.0, base=0,
                                        pattern=[[0, G], [1, P]], channel_multiplier=-1).then_inc(mask_done, 1)

            def divide(i, c):
                pool.wait_ge(rsum_done, NC * i + c + 1)
                nc.gpsimd.tensor_tensor(yt[:, c % 2], ot[:, c % 2],
                                        rsum[:, c % 2, :].unsqueeze(2).to_broadcast([P, CH // 32, 32]), ALU.mult
                                        ).then_inc(yt_done, 1)

            def y_split(i, c):
                pool.wait_ge(yhi_done, NC * i + c + 1)
                nc.gpsimd.tensor_tensor(y_lo[:, c % 2], y_sb[:, c % 2], y_hi[:, c % 2], ALU.subtract).then_inc(ylo_done, 1)

            def iteration(i, first=False):
                for s in range(NS):
                    if is_diagonal(s):
                        mask_step(i, s)
                    if s == 1 and not first:
                        divide(i - 1, NC - 1)
                    if s == 5 and not first:
                        y_split(i - 1, NC - 1)
                    for c in range(NC - 1):
                        if s == CHUNK_END[c] + 3:
                            divide(i, c)
                        if s == CHUNK_END[c] + 7:
                            y_split(i, c)

            pool.wait_ge(w_in, 16 * len(w_f))
            for q, (f, (hi, lo)) in enumerate(zip(w_f, weights)):
                flat = "p k n -> p (k n)"
                f, hi, lo = f[:].rearrange(flat), hi[:].rearrange(flat), lo[:].rearrange(flat)
                nc.gpsimd.tensor_scalar(f, f, SX, None, ALU.mult).then_inc(w_scaled, 1)
                pool.wait_ge(w_scaled, q + 1)
                nc.gpsimd.tensor_copy(hi, f).then_inc(whi_done, 1)
                pool.wait_ge(whi_done, q + 1)
                nc.gpsimd.tensor_tensor(lo, f, hi, ALU.subtract).then_inc(w_done, 1)
            iteration(0, first=True)
            with pool.Fori(1, NIT) as i:
                iteration(i)
            divide(NIT - 1, NC - 1)
            y_split(NIT - 1, NC - 1)


def stage3(nc, x, att_d, weights, b1, b2, ident_d, out):
    with ExitStack() as ctx:
        def sb(name, shape, dt):
            return ctx.enter_context(nc.sbuf_tensor(name, shape, dt))

        def sem(name):
            return ctx.enter_context(nc.semaphore(name))

        (wo_hi, wo_lo), (w1_hi, w1_lo), (w2_hi, w2_lo) = weights
        ident = sb("s3_ident", [P, P], F32)
        b1_in = sb("s3_b1_in", [P, KF], F32)
        b1_s = sb("s3_b1_s", [P, KF], F32)
        b2_all = sb("s3_b2_all", [P, D], F32)
        eps = sb("s3_eps", [P, 1], F32)
        xin = sb("s3_xin", [P, 2, TPC, D], F32)
        att_hi, att_lo = sb("s3_att_hi", [P, 2, KD, CH], F16), sb("s3_att_lo", [P, 2, KD, CH], F16)
        x2 = sb("s3_x2", [P, 2, TPC, D], F32)
        x2b = sb("s3_x2b", [P, 2, TPC, D], F32)
        xn = sb("s3_xn", [P, 2, TPC, D], F32)
        stats = sb("s3_stats", [P, 2, TPC, 6], F32)
        mv = sb("s3_mv", [P, 2, TPC, 2], F32)
        std = sb("s3_std", [P, 2, TPC], F32)
        rstd = sb("s3_rstd", [P, 2, TPC], F32)
        xt_hi, xt_lo = sb("s3_xt_hi", [P, 2, KD, CH], F16), sb("s3_xt_lo", [P, 2, KD, CH], F16)
        h_f = sb("s3_h_f", [P, 2, CH], F32)
        h_hi, h_lo = sb("s3_h_hi", [P, 2, KF, CH], F16), sb("s3_h_lo", [P, 2, KF, CH], F16)
        y = sb("s3_y", [P, 2, TPC, D], F32)
        ps = ctx.enter_context(nc.psum_tensor("s3_ps", [P, 8, CH], F32))
        A_BANK, XT_BANK, H_BANK, Y_BANK = 0, 2, 4, 6

        w_in, preset, aggregating = sem("s3_w_in"), sem("s3_preset"), sem("s3_aggregating")
        x_in = [sem(f"s3_x_in{p}") for p in range(2)]
        att_in = [sem(f"s3_att_in{p}") for p in range(2)]
        a_ready, x2_done, x2b_done = sem("s3_a_ready"), sem("s3_x2_done"), sem("s3_x2b_done")
        stats_done, mv_done, std_done = sem("s3_stats_done"), sem("s3_mv_done"), sem("s3_std_done")
        rstd_done, xn_done = sem("s3_rstd_done"), sem("s3_xn_done")
        xt_ready, xhi_done, xlo_done = sem("s3_xt_ready"), sem("s3_xhi_done"), sem("s3_xlo_done")
        h_ready, h_done, hhi_done, hlo_done = sem("s3_h_ready"), sem("s3_h_done"), sem("s3_hhi_done"), sem("s3_hlo_done")
        y_ready, y_done = sem("s3_y_ready"), sem("s3_y_done")
        y_out = [sem(f"s3_y_out{p}") for p in range(2)]
        NPAIR = NCHUNK // 2

        block = ctx.enter_context(nc.Block())

        @block.sync
        def _(sp):
            def load_x(n, p):
                sp.dma_start(xin[:, p], x[bass.ds(n * CH, CH), :].rearrange("(t p) d -> p t d", p=P)
                             ).then_inc(x_in[p], 16)

            def load_att(b, cc, p):
                for dst, hl in ((att_hi, 0), (att_lo, 1)):
                    for g in range(NG):
                        src = att_d[hl, bass.ds(NG * b + g, 1), :, cc * CH:(cc + 1) * CH].rearrange(
                            "a (j r) t -> (a j) r t", r=2 * DK)[:, 0:DK, :]
                        sp.dma_start(dst[GC * (g % 2):GC * (g % 2 + 1), p, g // 2, :], src).then_inc(att_in[p], 16)

            def step(b, cc, last):
                n, p = NC * b + cc, cc % 2
                if not (last and cc >= NC - 2):
                    sp.wait_ge(x2_done, 2 * (n + 1) + 2)
                    load_x(n + 2, p)
                    if cc + 2 < NC:
                        load_att(b, cc + 2, p)
                    else:
                        load_att(b + 1, cc + 2 - NC, p)
                for pair in range(2):
                    sp.wait_ge(y_done, 2 * n + pair + 1 + 2)
                    sp.dma_start(out[bass.ds(n * CH + pair * 2 * P, 2 * P), :].rearrange("(t p) d -> p t d", p=P),
                                 y[:, p, 2 * pair:2 * pair + 2]).then_inc(y_out[p], 16)

            load_x(0, 0)
            load_att(0, 0, 0)
            sp.dma_start(ident[:], ident_d).then_inc(w_in, 16)
            sp.dma_start(b1_in[:], b1).then_inc(w_in, 16)
            sp.dma_start(b2_all[:], b2.rearrange("(a d) -> a d", a=1).to_broadcast([P, D])).then_inc(w_in, 16)
            load_x(1, 1)
            load_att(0, 1, 1)
            with sp.Fori(0, B - 1) as b:
                for cc in range(NC):
                    step(b, cc, False)
            for cc in range(NC):
                step(B - 1, cc, True)
            for p in range(2):
                sp.wait_ge(y_out[p], 32 * (NPAIR + 1))

        @block.tensor
        def _(pe):
            def project(n, p, use):
                pe.wait_ge(att_in[p], 16 * 2 * NG * (use + 1))
                for pair in range(2):
                    pe.wait_ge(x2_done, 2 * n + pair + 1)
                    for t in range(2):
                        tt = 2 * pair + t
                        mm = [(a, w, k) for a, w in terms(att_hi, att_lo, wo_hi, wo_lo) for k in range(KD)]
                        for q, (a, w, k) in enumerate(mm):
                            last = nc.tensor.matmul(ps[:, A_BANK + pair, t * D:(t + 1) * D],
                                                    a[:, p, k, tt * P:(tt + 1) * P], w[:, k],
                                                    start=q == 0, stop=q == len(mm) - 1)
                    last.then_inc(a_ready, 1)

            def transposes(n, p):
                pe.wait_ge(xn_done, n + 1)
                pe.wait_ge(xlo_done, n)
                for k in range(KD):
                    for t in range(TPC):
                        last = nc.tensor.transpose(ps[:, XT_BANK + k, t * P:(t + 1) * P],
                                                   xn[:, p, t, k * P:(k + 1) * P], ident[:])
                last.then_inc(xt_ready, 1)

            def ffn1(n, p):
                pe.wait_ge(xlo_done, n + 1)
                for f in range(KF):
                    pe.wait_ge(h_done, KF * n + f + 1)
                    mm = [(w, a, k) for w, a in terms(w1_hi, w1_lo, xt_hi, xt_lo) for k in range(KD)]
                    for q, (w, a, k) in enumerate(mm):
                        last = nc.tensor.matmul(ps[:, H_BANK + f % 2], w[:, k, f * P:(f + 1) * P], a[:, p, k],
                                                start=q == 0, stop=q == len(mm) - 1)
                    last.then_inc(h_ready, 1)

            def ffn2_tile(n, p, tt):
                pair, t = divmod(tt, 2)
                if t == 0:
                    pe.wait_ge(y_done, 2 * n + pair + 1)
                mm = [(a, w, k) for k in range(KF) for a, w in terms(h_hi, h_lo, w2_hi, w2_lo)]
                for q, (a, w, k) in enumerate(mm):
                    last = nc.tensor.matmul(ps[:, Y_BANK + pair, t * D:(t + 1) * D],
                                            a[:, p, k, tt * P:(tt + 1) * P], w[:, k],
                                            start=q == 0, stop=q == len(mm) - 1)
                if t == 1:
                    last.then_inc(y_ready, 1)

            def step(n, p, next_use, last=False):
                ffn1(n, p)
                if not last:
                    project(n + 1, 1 - p, next_use)
                pe.wait_ge(hlo_done, KF * (n + 1) + 2)
                for tt in range(TPC):
                    if tt == TPC - 1 and not last:
                        transposes(n + 1, 1 - p)
                    ffn2_tile(n, p, tt)

            pe.wait_ge(w_in, 48)
            project(0, 0, 0)
            transposes(0, 0)
            with pe.Fori(0, NPAIR - 1) as u:
                step(2 * u, 0, u)
                step(2 * u + 1, 1, u + 1)
            step(NCHUNK - 2, 0, NPAIR - 1)
            step(NCHUNK - 1, 1, 0, last=True)

        @block.vector
        def _(dve):
            def residual(n, p, use):
                dve.wait_ge(x_in[p], 16 * (use + 1))
                for pair in range(2):
                    dve.wait_ge(a_ready, 2 * n + pair + 1)
                    dve.wait_ge(x2b_done, n + 1)
                    nc.vector.scalar_tensor_tensor(x2[:, p, 2 * pair:2 * pair + 2].rearrange("p t d -> p (t d)"),
                                                   ps[:, A_BANK + pair], 1.0 / SQK,
                                                   xin[:, p, 2 * pair:2 * pair + 2].rearrange("p t d -> p (t d)"),
                                                   ALU.mult, ALU.add).then_inc(x2_done, 1)

            def statistics(n, p):
                dve.wait_ge(x2_done, 2 * (n + 1) + 2)
                for t in range(TPC):
                    nc.vector.bn_stats(stats[:, p, t, :], x2[:, p, t, :]).then_inc(stats_done, 1)

            def normalize(n, p):
                dve.wait_ge(stats_done, TPC * (n + 1))
                dve.sem_inc(aggregating, 1)
                for t in range(TPC):
                    last = nc.vector.bn_aggr(mv[:, p, t, :], stats[:, p, t, :])
                last.then_inc(mv_done, 1)
                dve.wait_ge(std_done, n + 1)
                nc.vector.reciprocal(rstd[:, p, :], std[:, p, :]).then_inc(rstd_done, 1)
                dve.wait_ge(rstd_done, n + 1)
                for t in range(TPC):
                    last = nc.vector.tensor_scalar(xn[:, p, t, :], x2[:, p, t, :], mv[:, p, t, 0:1],
                                                   rstd[:, p, t:t + 1], ALU.subtract, ALU.mult)
                last.then_inc(xn_done, 1)

            def split_xt(n, p):
                dve.wait_ge(xhi_done, n + 1)
                for k in range(KD):
                    last = nc.vector.tensor_tensor(xt_lo[:, p, k], ps[:, XT_BANK + k], xt_hi[:, p, k], ALU.subtract)
                last.then_inc(xlo_done, 1)

            def split_h(n, p, f):
                dve.wait_ge(h_done, KF * n + f + 1 + 2)
                nc.vector.tensor_copy(h_hi[:, p, f], h_f[:, f % 2]).then_inc(hhi_done, 1)
                dve.wait_ge(hhi_done, KF * n + f + 1)
                nc.vector.tensor_tensor(h_lo[:, p, f], h_f[:, f % 2], h_hi[:, p, f], ALU.subtract).then_inc(hlo_done, 1)

            def output(n, p, use, pair):
                dve.wait_ge(y_ready, 2 * n + pair + 1)
                dve.wait_ge(x2b_done, n + 1 + 2)
                dve.wait_ge(y_out[p], 32 * (use + 1))
                nc.vector.scalar_tensor_tensor(y[:, p, 2 * pair:2 * pair + 2].rearrange("p t d -> p (t d)"),
                                               ps[:, Y_BANK + pair], 1.0 / (SH * SX),
                                               x2b[:, p, 2 * pair:2 * pair + 2].rearrange("p t d -> p (t d)"),
                                               ALU.mult, ALU.add).then_inc(y_done, 1)

            def step(n, p, use, next_use, last=False):
                for f in range(KF):
                    split_h(n, p, f)
                if not last:
                    residual(n + 1, 1 - p, next_use)
                    statistics(n + 1, 1 - p)
                    normalize(n + 1, 1 - p)
                output(n, p, use, 0)
                if not last:
                    split_xt(n + 1, 1 - p)
                output(n, p, use, 1)

            dve.sem_inc(x2b_done, 2)
            dve.sem_inc(y_done, 2)
            for p in range(2):
                dve.sem_inc(y_out[p], 32)
            dve.sem_inc(x2_done, 2)
            dve.sem_inc(hlo_done, 2)
            nc.vector.memset(eps[:], EPS / SX ** 2).then_inc(preset, 1)
            dve.wait_ge(w_in, 48)
            nc.vector.tensor_scalar(b1_s[:], b1_in[:], SH, None, ALU.mult).then_inc(preset, 1)
            residual(0, 0, 0)
            statistics(0, 0)
            normalize(0, 0)
            split_xt(0, 0)
            with dve.Fori(0, NPAIR - 1) as u:
                step(2 * u, 0, u, u)
                step(2 * u + 1, 1, u, u + 1)
            step(NCHUNK - 2, 0, NPAIR - 1, NPAIR - 1)
            step(NCHUNK - 1, 1, NPAIR - 1, 0, last=True)

        @block.scalar
        def _(act):
            def std_of(n, p):
                act.wait_ge(mv_done, n + 1)
                nc.scalar.activation(std[:, p, :], mv[:, p, :, 1], ACT.Sqrt, bias=eps[:], scale=1.0 / SX ** 2
                                     ).then_inc(std_done, 1)

            def hi_xt(n, p):
                act.wait_ge(xt_ready, n + 1)
                for k in range(KD):
                    last = nc.scalar.copy(xt_hi[:, p, k], ps[:, XT_BANK + k])
                last.then_inc(xhi_done, 1)

            def relu(n, f):
                act.wait_ge(h_ready, KF * n + f + 1)
                act.wait_ge(hlo_done, KF * n + f + 1)
                nc.scalar.activation(h_f[:, f % 2], ps[:, H_BANK + f % 2], ACT.Relu, bias=b1_s[:, f:f + 1],
                                     scale=SH / SQK).then_inc(h_done, 1)

            def step(n, p, last=False):
                for f in range(KF):
                    relu(n, f)
                if not last:
                    std_of(n + 1, 1 - p)
                    hi_xt(n + 1, 1 - p)

            act.sem_inc(h_done, 2)
            act.wait_ge(preset, 2)
            std_of(0, 0)
            hi_xt(0, 0)
            with act.Fori(0, NPAIR - 1) as u:
                step(2 * u, 0)
                step(2 * u + 1, 1)
            step(NCHUNK - 2, 0)
            step(NCHUNK - 1, 1, last=True)

        @block.gpsimd
        def _(pool):
            def add_b2(n, p):
                pool.wait_ge(x2_done, 2 * (n + 1) + 2)
                if not isinstance(n, int) or n > 1:
                    pool.wait_ge(y_done, 2 * n)
                for t in range(TPC):
                    last = nc.gpsimd.tensor_tensor(x2b[:, p, t], x2[:, p, t], b2_all[:], ALU.add)
                last.then_inc(x2b_done, 1)

            pool.wait_ge(w_in, 48)
            add_b2(0, 0)
            add_b2(1, 1)
            with pool.Fori(1, NPAIR) as u:
                add_b2(2 * u, 0)
                add_b2(2 * u + 1, 1)


def layer(nc, x, wqkv, wo, w1, b1, w2, b2, cos_d, sin_d, ident_d, mask_d, out):
    qk_d = nc.dram_tensor("qk_scratch", (NIT, 2, 2, GC, S), F16, kind="Internal").ap()
    v_d = nc.dram_tensor("v_scratch", (P, S // P, NIT, G * 2 * DK), F32, kind="Internal").ap()
    att_d = nc.dram_tensor("att_scratch", (2, NIT, P, S), F16, kind="Internal").ap()
    with ExitStack() as ctx:
        weights = [[ctx.enter_context(nc.sbuf_tensor(f"{name}_{part}", [P, k, n], F16)) for part in ("hi", "lo")]
                   for name, k, n in (("wo", KD, D), ("w1", KD, F), ("w2", KF, D))]
        with ExitStack() as attention:
            ops = Operands(nc, attention)
            stage1(nc, x, wqkv, cos_d, sin_d, ident_d, qk_d, v_d, ops)
            stage2(nc, ident_d, mask_d, qk_d, v_d, att_d, (wo, w1, w2), weights, ops)
        stage3(nc, x, att_d, weights, b1, b2, ident_d, out)


def shape_constants():
    freqs = (1.0 / np.float32(10000.0) ** (np.arange(0, DK, 2, dtype=np.float32) / np.float32(DK))).astype(np.float32)
    angles = freqs[(np.arange(P) % DK) // 2][:, None] * np.arange(S, dtype=np.float32)[None, :]
    sign = np.where(np.arange(P) % 2 == 0, -1.0, 1.0)[:, None]
    cos = (np.cos(angles) / SX).astype(np.float32)
    sin = (np.sin(angles) * sign / SX).astype(np.float32)
    r = np.arange(P)
    mask = np.concatenate([np.zeros((P, CH - P)), np.where(r[None, :] > r[:, None], MASKED, 0.0)], axis=1)
    return {"cos": cos, "sin": sin, "ident": np.eye(P, dtype=np.float32), "mask": mask.astype(np.float32)}


def kernel(L0_attn_x, L0_attn_Wq, L0_attn_Wk, L0_attn_Wv, L0_attn_Wo, L0_ffn_w1, L0_ffn_b1, L0_ffn_w2, L0_ffn_b2):
    import concourse.bacc as bacc
    from concourse.bass_utils import run_bass_kernel_spmd

    wq, wk, wv, wo = (np.asarray(w).T for w in (L0_attn_Wq, L0_attn_Wk, L0_attn_Wv, L0_attn_Wo))
    cols = []
    for g in range(NG):
        cols += [wq[:, GC * g:GC * (g + 1)], wk[:, GC * g:GC * (g + 1)]]
    arrays = {
        "x": np.asarray(L0_attn_x).reshape(B * S, D),
        "w_qkv": np.concatenate(cols + [wv], axis=1),
        "w_o": wo,
        "w_1": np.asarray(L0_ffn_w1), "b_1": np.asarray(L0_ffn_b1).reshape(KF, P).T,
        "w_2": np.asarray(L0_ffn_w2), "b_2": np.asarray(L0_ffn_b2),
        **shape_constants(),
    }
    arrays = {name: np.ascontiguousarray(a) for name, a in arrays.items()}
    nc = bacc.Bacc("TRN2", target_bir_lowering=False, num_devices=1)
    args = [nc.dram_tensor(name, a.shape, mybir.dt.from_np(a.dtype), kind="ExternalInput").ap()
            for name, a in arrays.items()]
    out = nc.dram_tensor("out", (B * S, D), F32, kind="ExternalOutput").ap()
    layer(nc, *args, out)
    r = run_bass_kernel_spmd(nc, [arrays], core_ids=[0])
    return r.results[0]["out"].reshape(B, S, D)
```

```python
from contextlib import ExitStack

import numpy as np

import concourse.bass as bass
from concourse import mybir

ALU = mybir.AluOpType
ACT = mybir.ActivationFunctionType
AX = mybir.AxisListType
F32 = mybir.dt.float32
F16 = mybir.dt.float16

P = 128
B, S, D, H, F = 4, 2048, 256, 16, 1024
DK = D // H
CH = 512
NC = S // CH
TPC = CH // P
NCHUNK = B * NC
KD = D // P
KF = F // P
G = 4
NG = H // G
GC = G * DK
NIT = B * NG
EPS = 1e-5

SX = 64.0
SH = 16.0
SQK = SX * SX

ROLE_ROWS = 3 * DK
MAXROW = ROLE_ROWS
HROWS = 64
MROWS = 32 * (G - 1) + DK
AROWS = HROWS + MAXROW + 1

STEPS = [(c, kb) for c in range(NC) for kb in range(TPC * (c + 1))]
NS = len(STEPS)
CHUNK_END = [max(s for s in range(NS) if STEPS[s][0] == c) for c in range(NC)]
CHUNK_START = [min(s for s in range(NS) if STEPS[s][0] == c) for c in range(NC)]
HALF_STEP = CHUNK_END[NC // 2 - 1] + 1
UNITS = G * NS
NDIAG = NC * TPC
MASKED = -1e30


def is_diagonal(s):
    c, kb = STEPS[s]
    return kb >= TPC * c


def diagonals(s):
    return sum(is_diagonal(t) for t in range(s))


def terms(a_hi, a_lo, b_hi, b_lo):
    return ((a_hi, b_hi), (a_hi, b_lo), (a_lo, b_hi))


def load_m(sp, ops, qk_d, i, p):
    for j in range(G):
        rows = slice(32 * j, 32 * j + DK)
        for qk, dst in ((0, ops.mq[rows, p, j]), (1, ops.mk[rows, p])):
            src = qk_d[bass.ds(i, 1), qk, 0, DK * j:DK * (j + 1), :].rearrange("a r t -> (a r) t")
            sp.dma_start(dst, src).then_inc(ops.m_in[p], 16)


def load_a(sp, ops, qk_d, i, p):
    for qk, roles in ((0, (0, 1, 0)), (1, (0, 0, 1))):
        for r, hl in enumerate(roles):
            for jj in range(2):
                rows = slice(HROWS * jj + DK * r, HROWS * jj + DK * (r + 1))
                dst = ops.ak[rows, p] if qk else ops.aq[rows, p, jj:G:2]
                src = qk_d[bass.ds(i, 1), qk, hl].rearrange("a (jp jj r) t -> (a jj) r jp t", jj=2, r=DK)
                sp.dma_start(dst, src[jj]).then_inc(ops.a_in[p], 16)


def load_x(sp, ops, x, n, p):
    sp.dma_start(ops.xin[:, p], x[bass.ds(n * CH, CH), :].rearrange("(t p) d -> p t d", p=P)).then_inc(ops.x_in[p], 16)


def load_att(sp, ops, att_d, b, cc, p):
    for dst, hl in ((ops.att_hi, 0), (ops.att_lo, 1)):
        for g in range(NG):
            src = att_d[hl, bass.ds(NG * b + g, 1), :, cc * CH:(cc + 1) * CH].rearrange(
                "a (j r) t -> (a j) r t", r=2 * DK)[:, 0:DK, :]
            sp.dma_start(dst[GC * (g % 2):GC * (g % 2 + 1), p, g // 2, :], src).then_inc(ops.att_in[p], 16)


class Operands:
    def __init__(self, nc, ctx):
        self.mq = ctx.enter_context(nc.sbuf_tensor("mq", [P, 2, G, S], F16))
        self.mk = ctx.enter_context(nc.sbuf_tensor("mk", [P, 2, S], F16))
        self.aq = ctx.enter_context(nc.sbuf_tensor("aq", [P, 2, G, S], F16))
        self.ak = ctx.enter_context(nc.sbuf_tensor("ak", [P, 2, G // 2, S], F16))
        self.ident = ctx.enter_context(nc.sbuf_tensor("ident_sb", [P, P], F32))
        self.mask = ctx.enter_context(nc.sbuf_tensor("mask_sb", [P, CH], F32))
        self.const_in = ctx.enter_context(nc.semaphore("const_in"))
        self.xin = self.mq[:, 1, 0:2].rearrange("p j s -> p (j s)").bitcast(F32).rearrange(
            "p (b t d) -> p b t d", b=2, d=D)
        self.att_hi, self.att_lo = (self.mq[:, 0, j].rearrange("p (b k t) -> p b k t", b=2, t=CH) for j in range(2))
        self.x_in = [ctx.enter_context(nc.semaphore(f"x_in{p}")) for p in range(2)]
        self.att_in = [ctx.enter_context(nc.semaphore(f"att_in{p}")) for p in range(2)]
        self.m_in = [ctx.enter_context(nc.semaphore(f"m_in{p}")) for p in range(2)]
        self.a_in = [ctx.enter_context(nc.semaphore(f"a_in{p}")) for p in range(2)]


def stage1(nc, x, w_qkv, cos_d, sin_d, ident_d, mask_d, qk_d, v_d, ops):
    with ExitStack() as ctx:
        def sb(name, shape, dt):
            return ctx.enter_context(nc.sbuf_tensor(name, shape, dt))

        def sem(name):
            return ctx.enter_context(nc.semaphore(name))

        NW = 3 * D
        w_f = sb("s1_w_f", [P, KD, NW], F32)
        w_hi = sb("s1_w_hi", [P, KD, NW], F16)
        w_lo = sb("s1_w_lo", [P, KD, NW], F16)
        cos = sb("s1_cos", [P, S], F32)
        sin = sb("s1_sin", [P, S], F32)
        eps = sb("s1_eps", [P, 1], F32)
        xin = sb("s1_xin", [P, 2, TPC, D], F32)
        xn = sb("s1_xn", [P, 2, TPC, D], F32)
        stats = sb("s1_stats", [P, 2, TPC, 6], F32)
        mv = sb("s1_mv", [P, 2, TPC, 2], F32)
        negmean = sb("s1_negmean", [P, 2, TPC], F32)
        std = sb("s1_std", [P, 2, TPC], F32)
        rstd = sb("s1_rstd", [P, 2, TPC], F32)
        xt_hi = sb("s1_xt_hi", [P, 2, KD, CH], F16)
        xt_lo = sb("s1_xt_lo", [P, 2, KD, CH], F16)
        rot_a = sb("s1_rot_a", [P, NG, CH], F32)
        rot_b = sb("s1_rot_b", [P, NG, CH], F32)
        r_hi = sb("s1_r_hi", [P, NG, CH], F16)
        r_lo = sb("s1_r_lo", [P, NG, CH], F16)
        vst = sb("s1_vst", [P, 2, 2, H, 2 * DK], F32)
        ps = ctx.enter_context(nc.psum_tensor("s1_ps", [P, 8, CH], F32))
        XT_BANK, QK_BANK, V_BANK = 0, 2, 6

        ident_in, w_in, trig_in = sem("s1_ident_in"), sem("s1_w_in"), sem("s1_trig_in")
        whi_done, w_done = sem("s1_whi_done"), sem("s1_w_done")
        eps_preset, v_preset, ops_preset = sem("s1_eps_preset"), sem("s1_v_preset"), sem("s1_ops_preset")
        x_in = [sem(f"s1_x_in{p}") for p in range(2)]
        stats_done, mv_done, std_done = sem("s1_stats_done"), sem("s1_mv_done"), sem("s1_std_done")
        aggregating, mean_done = sem("s1_aggregating"), sem("s1_mean_done")
        rstd_done, centred, xn_done = sem("s1_rstd_done"), sem("s1_centred"), sem("s1_xn_done")
        xt_ready, xhi_done, xlo_done = sem("s1_xt_ready"), sem("s1_xhi_done"), sem("s1_xlo_done")
        qk_ready, v_ready = sem("s1_qk_ready"), sem("s1_v_ready")
        rot_read, rotsin_done, rot_done = sem("s1_rot_read"), sem("s1_rotsin_done"), sem("s1_rot_done")
        rhi_done, rlo_done = sem("s1_rhi_done"), sem("s1_rlo_done")
        v_copied = sem("s1_v_copied")
        qk_out = [sem(f"s1_qk_out{g}") for g in range(NG)]
        v_out = [sem(f"s1_v_out{pair}") for pair in range(2)]

        block = ctx.enter_context(nc.Block())

        MANY = NC + 1

        def steps(step, engine):
            for cc in range(NC):
                step(cc, cc, 0, cc == 0, MANY)
            with engine.Fori(1, B - 1) as b:
                for cc in range(NC):
                    step(NC * b + cc, cc, b, False, MANY)
            for cc in range(NC):
                step(NCHUNK - NC + cc, cc, B - 1, False, NC - cc)

        @block.sync
        def _(sp):
            def load_x(n, p):
                sp.dma_start(xin[:, p], x[bass.ds(n * CH, CH), :].rearrange("(t p) d -> p t d", p=P)
                             ).then_inc(x_in[p], 16)

            for g in range(NG):
                sp.sem_inc(qk_out[g], 32)
            for pair in range(2):
                sp.sem_inc(v_out[pair], 16)
            load_x(0, 0)
            sp.dma_start(ops.ident[:], ident_d).then_inc(ident_in, 16)
            sp.dma_start(w_f[:], w_qkv.rearrange("(k p) n -> p k n", p=P)).then_inc(w_in, 16)
            load_x(1, 1)
            for dst, src in ((cos, cos_d), (sin, sin_d)):
                sp.dma_start(dst[:], src).then_inc(trig_in, 16)
            sp.dma_start(ops.mask[:], mask_d).then_inc(ops.const_in, 16)
            for n in range(2):
                sp.wait_ge(xn_done, n + 1)
                load_x(n + 2, n)

            def step(n, cc, b, first, left):
                for g in range(NG):
                    sp.wait_ge(rlo_done, NG * (n + 1) + g + 1)
                    for hl, src in ((1, r_lo), (0, r_hi)):
                        dst = qk_d[bass.ds(NG * b + g, 1), :, hl, :, cc * CH:(cc + 1) * CH].rearrange(
                            "a q r t -> (a q) r t")
                        sp.dma_start(dst, src[:, g, :]).then_inc(qk_out[g], 16)
                    if g == 1 and left > 4:
                        sp.wait_ge(xn_done, n + 3)
                        load_x(n + 4, cc % 2)
                for pair in range(2):
                    sp.wait_ge(v_copied, 2 * (n + 1) + pair + 1)
                    dst = v_d[:, TPC * cc + 2 * pair:TPC * cc + 2 * pair + 2, bass.ds(NG * b, NG), :].rearrange(
                        "p t g n -> p t (g n)")
                    sp.dma_start(dst, vst[:, pair].rearrange("p t h e -> p t (h e)")).then_inc(v_out[pair], 16)
                if left == NC:
                    sp.wait_ge(ops_preset, 4)
                    for i in range(2):
                        sp.wait_ge(qk_out[i], 32 * (NC + 1))
                        load_m(sp, ops, qk_d, i, i)
                if left == NC - 1:
                    load_a(sp, ops, qk_d, 0, 0)

            steps(step, sp)
            for g in range(NG):
                sp.wait_ge(qk_out[g], 32 * (NCHUNK + 1))
            for pair in range(2):
                sp.wait_ge(v_out[pair], 16 * (NCHUNK + 1))

        @block.tensor
        def _(pe):
            def transposes(n, p):
                pe.wait_ge(xn_done, n + 1)
                if not isinstance(n, int) or n > 0:
                    pe.wait_ge(xlo_done, n)
                for k in range(KD):
                    for t in range(TPC):
                        last = nc.tensor.transpose(ps[:, XT_BANK + k, t * P:(t + 1) * P],
                                                   xn[:, p, t, k * P:(k + 1) * P], ops.ident[:])
                last.then_inc(xt_ready, 1)

            def project_qk(n, p, g):
                pe.wait_ge(rot_read, NG * n + g + 1)
                mm = [(w, xt, k) for w, xt in terms(w_hi, w_lo, xt_hi, xt_lo) for k in range(KD)]
                for q, (w, xt, k) in enumerate(mm):
                    last = nc.tensor.matmul(ps[:, QK_BANK + g], w[:, k, 2 * GC * g:2 * GC * (g + 1)], xt[:, p, k],
                                            start=q == 0, stop=q == len(mm) - 1)
                last.then_inc(qk_ready, 1)

            def project_v(n, p):
                for pair in range(2):
                    pe.wait_ge(v_copied, 2 * n + pair + 1)
                    for t in range(2):
                        mm = [(xt, w, k) for xt, w in terms(xt_hi, xt_lo, w_hi, w_lo) for k in range(KD)]
                        for q, (xt, w, k) in enumerate(mm):
                            tt = 2 * pair + t
                            last = nc.tensor.matmul(ps[:, V_BANK + pair, t * D:(t + 1) * D],
                                                    xt[:, p, k, tt * P:(tt + 1) * P], w[:, k, 2 * D:3 * D],
                                                    start=q == 0, stop=q == len(mm) - 1)
                    last.then_inc(v_ready, 1)

            def step(n, cc, b, first, left):
                p = cc % 2
                pe.wait_ge(xlo_done, n + 1)
                project_qk(n, p, 0)
                project_qk(n, p, 1)
                if left > 1:
                    transposes(n + 1, 1 - p)
                project_qk(n, p, 2)
                project_qk(n, p, 3)
                project_v(n, p)

            pe.wait_ge(ident_in, 16)
            transposes(0, 0)
            pe.wait_ge(w_done, 1)
            steps(step, pe)

        @block.vector
        def _(dve):
            def statistics(n, p, use):
                dve.wait_ge(x_in[p], 16 * (use + 1))
                for t in range(TPC):
                    nc.vector.bn_stats(stats[:, p, t, :], xin[:, p, t, :]).then_inc(stats_done, 1)

            def aggregate(n, p):
                dve.wait_ge(stats_done, TPC * (n + 1))
                dve.sem_inc(aggregating, 1)
                for t in range(TPC):
                    last = nc.vector.bn_aggr(mv[:, p, t, :], stats[:, p, t, :])
                last.then_inc(mv_done, 1)
                dve.wait_ge(mv_done, n + 1)
                nc.vector.tensor_scalar(negmean[:, p, :], mv[:, p, :, 0], -1.0, None, ALU.mult).then_inc(mean_done, 1)

            def invert_std(n, p):
                dve.wait_ge(std_done, n + 1)
                nc.vector.reciprocal(rstd[:, p, :], std[:, p, :]).then_inc(rstd_done, 1)

            def split_xt(n, p):
                dve.wait_ge(xhi_done, n + 1)
                for k in range(KD):
                    last = nc.vector.tensor_tensor(xt_lo[:, p, k], ps[:, XT_BANK + k], xt_hi[:, p, k], ALU.subtract)
                last.then_inc(xlo_done, 1)

            def rope(n, cc, g):
                tok = slice(cc * CH, (cc + 1) * CH)
                dve.wait_ge(qk_ready, NG * n + g + 1)
                dve.wait_ge(rlo_done, NG * n + g + 1)
                nc.vector.tensor_tensor(rot_a[:, g], ps[:, QK_BANK + g], cos[:, tok], ALU.mult)
                nc.vector.stream_shuffle(rot_b[:, g], ps[:, QK_BANK + g], [r ^ 1 for r in range(32)]
                                         ).then_inc(rot_read, 1)

            def split_rot(n, g):
                dve.wait_ge(rhi_done, NG * n + g + 1)
                nc.vector.tensor_tensor(r_lo[:, g], rot_a[:, g], r_hi[:, g], ALU.subtract).then_inc(rlo_done, 1)

            def step(n, cc, b, first, left):
                p = cc % 2
                rope(n, cc, 0)
                if not first:
                    split_rot(n - 1, 2)
                rope(n, cc, 1)
                if not first:
                    split_rot(n - 1, 3)
                if left > 2:
                    statistics(n + 2, p, 2 * b + cc // 2 + 1)
                    aggregate(n + 2, p)
                rope(n, cc, 2)
                if left > 2:
                    invert_std(n + 2, p)
                if left > 1:
                    split_xt(n + 1, 1 - p)
                rope(n, cc, 3)
                split_rot(n, 0)
                split_rot(n, 1)

            dve.sem_inc(rot_read, NG)
            dve.sem_inc(rlo_done, NG)
            nc.vector.memset(eps[:], EPS / SX ** 2).then_inc(eps_preset, 1)
            for n in range(2):
                statistics(n, n, 0)
                aggregate(n, n)
                if n == 1:
                    nc.vector.memset(ops.ak[:].bitcast(F32), float(np.full(2, SQK, np.float16).view(np.float32)[0])
                                     ).then_inc(ops_preset, 1)
                invert_std(n, n)
            split_xt(0, 0)
            dve.wait_ge(whi_done, 1)
            nc.vector.scalar_tensor_tensor(w_lo[:].rearrange("p k n -> p (k n)"), w_f[:].rearrange("p k n -> p (k n)"),
                                           SX, w_hi[:].rearrange("p k n -> p (k n)"), ALU.mult, ALU.subtract
                                           ).then_inc(w_done, 1)
            dve.wait_ge(trig_in, 32)
            steps(step, dve)
            for g in (2, 3):
                split_rot(NCHUNK - 1, g)

        @block.gpsimd
        def _(pool):
            nc.gpsimd.memset(vst[:], 1.0 / SX).then_inc(v_preset, 1)
            for buffer in (ops.mq, ops.mk, ops.aq):
                nc.gpsimd.memset(buffer[:].bitcast(F32), 0.0).then_inc(ops_preset, 1)
            pool.wait_ge(trig_in, 32)
            with pool.Fori(0, B) as b:
                for cc in range(NC):
                    for g in range(NG):
                        u = NG * (NC * b + cc) + g
                        tok = slice(cc * CH, (cc + 1) * CH)
                        pool.wait_ge(rot_read, u + 1 + NG)
                        nc.gpsimd.tensor_tensor(rot_b[:, g], rot_b[:, g], sin[:, tok], ALU.mult).then_inc(rotsin_done, 1)
                        pool.wait_ge(rotsin_done, u + 1)
                        nc.gpsimd.tensor_tensor(rot_a[:, g], rot_a[:, g], rot_b[:, g], ALU.add).then_inc(rot_done, 1)

        @block.scalar
        def _(act):
            def std_of(n, p):
                act.wait_ge(mv_done, n + 1)
                nc.scalar.activation(std[:, p, :], mv[:, p, :, 1], ACT.Sqrt, bias=eps[:], scale=1.0 / SX ** 2
                                     ).then_inc(std_done, 1)

            def centre(n, p):
                act.wait_ge(mean_done, n + 1)
                if not isinstance(n, int) or n > 1:
                    act.wait_ge(xt_ready, n - 1)
                for t in range(TPC):
                    last = nc.scalar.activation(xn[:, p, t, :], xin[:, p, t, :], ACT.Identity, bias=negmean[:, p, t:t + 1])
                last.then_inc(centred, 1)

            def scale_rows(n, p):
                act.wait_ge(rstd_done, n + 1)
                act.wait_ge(centred, n + 1)
                for t in range(TPC):
                    last = nc.scalar.activation(xn[:, p, t, :], xn[:, p, t, :], ACT.Copy, scale=rstd[:, p, t:t + 1])
                last.then_inc(xn_done, 1)

            def hi_xt(n, p):
                act.wait_ge(xt_ready, n + 1)
                for k in range(KD):
                    last = nc.scalar.copy(xt_hi[:, p, k], ps[:, XT_BANK + k])
                last.then_inc(xhi_done, 1)

            def hi_rot(n, g):
                act.wait_ge(rot_done, NG * n + g + 1)
                act.wait_ge(qk_out[g], 32 * (n + 1))
                nc.scalar.copy(r_hi[:, g], rot_a[:, g]).then_inc(rhi_done, 1)

            def stage_v(n, pair):
                act.wait_ge(v_ready, 2 * n + pair + 1)
                act.wait_ge(v_out[pair], 16 * (n + 1))
                nc.scalar.activation(vst[:, pair, :, :, 0:DK],
                                     ps[:, V_BANK + pair].rearrange("p (t h e) -> p t h e", t=2, e=DK),
                                     ACT.Copy, scale=1.0 / SQK).then_inc(v_copied, 1)

            def step(n, cc, b, first, left):
                p = cc % 2
                if not first:
                    hi_rot(n - 1, 2)
                    stage_v(n - 1, 0)
                    hi_rot(n - 1, 3)
                    stage_v(n - 1, 1)
                if left > 1:
                    hi_xt(n + 1, 1 - p)
                if left > 2:
                    std_of(n + 2, p)
                    centre(n + 2, p)
                hi_rot(n, 0)
                if left > 2:
                    scale_rows(n + 2, p)
                hi_rot(n, 1)

            act.sem_inc(v_copied, 2)
            act.wait_ge(eps_preset, 1)
            for n in range(2):
                std_of(n, n)
                centre(n, n)
                scale_rows(n, n)
                if n == 0:
                    act.wait_ge(w_in, 16)
                    nc.scalar.activation(w_hi[:], w_f[:], ACT.Copy, scale=SX).then_inc(whi_done, 1)
                    hi_xt(0, 0)
            act.wait_ge(v_preset, 1)
            steps(step, act)
            hi_rot(NCHUNK - 1, 2)
            stage_v(NCHUNK - 1, 0)
            hi_rot(NCHUNK - 1, 3)
            stage_v(NCHUNK - 1, 1)


def stage2(nc, x, qk_d, v_d, att_d, weight_ds, weights, ops):
    with ExitStack() as ctx:
        def sb(name, shape, dt):
            return ctx.enter_context(nc.sbuf_tensor(name, shape, dt))

        def sem(name):
            return ctx.enter_context(nc.semaphore(name))

        ident, mask = ops.ident, ops.mask
        mq, mk, aq, ak, m_in, a_in = ops.mq, ops.mk, ops.aq, ops.ak, ops.m_in, ops.a_in
        v = sb("s2_v", [P, 2, S // P, G, 2 * DK], F32)
        part = sb("s2_part", [P, 2, G, 8, NC], F32)
        qmax = sb("s2_qmax", [P, 2, G * 8], F32)
        nrow = sb("s2_nrow", [G * 8, 2, P], F16)
        prob = sb("s2_prob", [P, 2, G, CH], F32)
        o_sb = sb("s2_o", [P, 2, CH], F32)
        ot = sb("s2_ot", [P, 2, CH // 32, 32], F32)
        rsum = sb("s2_rsum", [P, 2, CH // 32], F32)
        yt = sb("s2_yt", [P, 2, CH // 32, 32], F32)
        y_sb = sb("s2_y", [P, 2, CH], F32)
        y_hi = sb("s2_y_hi", [P, 2, CH], F16)
        y_lo = sb("s2_y_lo", [P, 2, CH], F16)
        w_f = [sb(f"s2_w{q}_f", hi.shape, F32) for q, (hi, lo) in enumerate(weights)]
        ps = ctx.enter_context(nc.psum_tensor("s2_ps", [P, 8, CH], F32))
        M_BANK, NM, S_BANK, SB, O_BANK = 0, 4, 4, 3, 7
        M_DMAS = 2 * G
        A_DMAS = 2 * 3 * 2

        part_preset = sem("s2_part_preset")
        v_in = [sem(f"s2_v_in{p}") for p in range(2)]
        m_ready, m_read = sem("s2_m_ready"), sem("s2_m_read")
        qmax_done = sem("s2_qmax_done")
        w_in, w_scaled, whi_done, w_done = sem("s2_w_in"), sem("s2_w_scaled"), sem("s2_whi_done"), sem("s2_w_done")
        masking, selecting = sem("s2_masking"), sem("s2_selecting")
        rows_in = [sem(f"s2_rows_in{h}") for h in range(2)]
        s_ready, p_done, mask_done = sem("s2_s_ready"), sem("s2_p_done"), sem("s2_mask_done")
        pv_done, o_copied = sem("s2_pv_done"), sem("s2_o_copied")
        ot_done, rsum_done, yt_done = sem("s2_ot_done"), sem("s2_rsum_done"), sem("s2_yt_done")
        y_done, yhi_done, ylo_done = sem("s2_y_done"), sem("s2_yhi_done"), sem("s2_ylo_done")
        y_out = [sem(f"s2_y_out{p}") for p in range(2)]

        M_BEFORE, M_ITER = UNITS + 1, UNITS + 2
        ROWS2_STEP, ROWS1_STEP = CHUNK_START[1] + 1, HALF_STEP + 1
        TURN_STEP = [CHUNK_START[2] + 2, CHUNK_START[2] + 5, CHUNK_START[3] + 3, CHUNK_START[1] + 1]
        BACK, SPLIT = 2, 4
        LATE = NC - 1
        ST = UNITS

        def m_use(i, s, j):
            return M_BEFORE + i * M_ITER + G * s + j + (s > ROWS2_STEP) + (s > ROWS1_STEP)

        def rows_use(i, half):
            s = (ROWS1_STEP, ROWS2_STEP)[half]
            return M_BEFORE + i * M_ITER + G * (s + 1) + (half == 0)

        assert 2 * M_ITER % NM == 0

        def bank_of(p, local):
            return M_BANK + (M_BEFORE + p * M_ITER + local) % NM

        def m_bank(p, s, j):
            return bank_of(p, G * s + j + (s > ROWS2_STEP) + (s > ROWS1_STEP))

        def rows_bank(p, half):
            s = (ROWS1_STEP, ROWS2_STEP)[half]
            return bank_of(p, G * (s + 1) + (half == 0))

        def second_rows_use(i, last):
            return M_BEFORE + i * M_ITER if last else rows_use(i, 1)

        def second_rows_bank(p, last):
            return bank_of(p, 0) if last else rows_bank(p, 1)

        def s_bank(s, j):
            return S_BANK + (G * s + j) % SB

        def read_before(i, s, j):
            u = G * s + j
            last_in_bank = u - SB if u >= SB else max(t for t in range(ST) if t % SB == u) - ST
            return ST * i + last_in_bank + 1

        def qtile(s):
            c, kb = STEPS[s]
            if is_diagonal(s):
                return TPC * (c + 1) - 1 - (kb - TPC * c), c
            return TPC * c + kb // c, kb % c

        block = ctx.enter_context(nc.Block())

        @block.sync
        def _(sp):
            def load_v(i, p):
                sp.dma_start(v[:, p].rearrange("p k j e -> p k (j e)"),
                             v_d[:, :, bass.ds(i, 1), :].rearrange("p k a n -> p k (a n)")).then_inc(v_in[p], 16)

            def rows(i, p, half, use):
                sp.wait_ge(m_read, NM + use + 1)
                for j in range(G):
                    row = HROWS * (j % 2) + MAXROW
                    sp.dma_start(aq[row:row + 1, p, j, half * S // 2:(half + 1) * S // 2],
                                 nrow[8 * j:8 * j + 8, half, :]).then_inc(rows_in[half], 16)

            def store(i, c):
                sp.wait_ge(ylo_done, NC * i + c + 1 + 2)
                for hl, src in ((1, y_lo), (0, y_hi)):
                    dst = att_d[hl, bass.ds(i, 1), :, c * CH:(c + 1) * CH].rearrange("a p t -> (a p) t")
                    sp.dma_start(dst, src[:, c % 2]).then_inc(y_out[c % 2], 16)

            def iteration(i, p, first=False, last=False, load2=True):
                if load2:
                    sp.wait_ge(m_ready, M_BEFORE + i * M_ITER)
                    load_m(sp, ops, qk_d, i + 2, p)
                rows(i, p, 1, second_rows_use(i, last))
                if not first:
                    store(i - 1, NC - 1)
                if not last:
                    if not first:
                        sp.wait_ge(pv_done, NS * i + 2)
                    load_a(sp, ops, qk_d, i + 1, 1 - p)
                    load_v(i + 1, 1 - p)
                store(i, 0)
                if not last:
                    rows(i + 1, 1 - p, 0, rows_use(i, 0))
                if last:
                    sp.wait_ge(m_ready, M_BEFORE + i * M_ITER)
                    for q in range(2):
                        sp.wait_ge(y_out[q], 32 * NG * NC // 2)
                    for n in range(2):
                        load_x(sp, ops, x, n, n)
                        load_att(sp, ops, att_d, 0, n, n)
                store(i, 1)
                store(i, 2)

            load_v(0, 0)
            for dst, src in zip(w_f, weight_ds):
                sp.dma_start(dst[:], src.rearrange("(k p) n -> p k n", p=P)).then_inc(w_in, 16)
            rows(0, 0, 0, M_BEFORE - 1)
            iteration(0, 0, first=True)
            with sp.Fori(1, NIT - 3, 2) as i:
                iteration(i, 1)
                iteration(i + 1, 0)
            iteration(NIT - 3, 1)
            iteration(NIT - 2, 0, load2=False)
            iteration(NIT - 1, 1, last=True, load2=False)
            store(NIT - 1, NC - 1)
            for p in range(2):
                sp.wait_ge(y_out[p], 16 * 2 * NIT * NC // 2)

        @block.tensor
        def _(pe):
            def max_tile(p, s, j, use, bank):
                qt, kc = qtile(s)
                w = min(CH, (qt + 1) * P - kc * CH)
                pe.wait_ge(m_read, use + 1)
                nc.tensor.matmul(ps[:, bank, 0:w], mq[0:MROWS, p, j, qt * P:(qt + 1) * P],
                                 mk[0:MROWS, p, kc * CH:kc * CH + w], start=True, stop=True).then_inc(m_ready, 1)

            def max_rows(half, use, bank, qmax_count):
                pe.wait_ge(qmax_done, qmax_count)
                pe.wait_ge(m_read, use + 1)
                nc.tensor.transpose(ps[0:G * 8, bank, 0:P], qmax[:, half, :], ident[:]).then_inc(m_ready, 1)

            def score_tile(i, p, s, j):
                c, kb = STEPS[s]
                q0 = max(0, kb - TPC * c) * P
                pe.wait_ge(p_done, G + read_before(i, s, j))
                nc.tensor.matmul(ps[:, s_bank(s, j), q0:CH], ak[0:AROWS, p, j // 2, kb * P:(kb + 1) * P],
                                 aq[0:AROWS, p, j, c * CH + q0:(c + 1) * CH], start=True, stop=True
                                 ).then_inc(s_ready, 1)

            def pv_step(i, p, s):
                c, kb = STEPS[s]
                q0 = max(0, kb - TPC * c) * P
                if kb == 0:
                    pe.wait_ge(o_copied, NC * i + c)
                if is_diagonal(s):
                    pe.wait_ge(mask_done, G * (NDIAG * i + diagonals(s) + 1))
                else:
                    pe.wait_ge(p_done, ST * i + G * s + G + G)
                for j in range(G):
                    last = nc.tensor.matmul(ps[32 * j:32 * j + 32, O_BANK, q0:CH], v[:, p, kb, j, :],
                                            prob[:, s % 2, j, q0:CH], start=kb == 0, stop=kb == TPC * (c + 1) - 1)
                last.then_inc(pv_done, 1)

            def iteration(i, p, use, first=False, last=False):
                pe.wait_ge(a_in[p], A_DMAS * 16 * (use + 1))
                pe.wait_ge(v_in[p], 16 * (use + 1))
                pe.wait_ge(rows_in[0], 16 * G * (i + 1))
                for s in range(NS):
                    if s == HALF_STEP:
                        pe.wait_ge(rows_in[1], 16 * G * (i + 1))
                    for j in range(G):
                        score_tile(i, p, s, j)
                        if not last:
                            if s == 0 and j == 0:
                                pe.wait_ge(m_in[1 - p], M_DMAS * 16 * (use + (1 if p else 0) + 1))
                            max_tile(1 - p, s, j, m_use(i, s, j), m_bank(p, s, j))
                    if s > 0:
                        pv_step(i, p, s - 1)
                    elif not first:
                        pv_step(i - 1, 1 - p, NS - 1)
                    if s == ROWS2_STEP:
                        max_rows(1, second_rows_use(i, last), second_rows_bank(p, last),
                                 2 * i + 2)
                    if s == ROWS1_STEP and not last:
                        max_rows(0, rows_use(i, 0), rows_bank(p, 0), 2 * i + 3)

            pe.wait_ge(m_in[0], M_DMAS * 16)
            for s in range(NS):
                for j in range(G):
                    use = G * s + j + (s > ROWS1_STEP)
                    max_tile(0, s, j, use, M_BANK + use % NM)
                if s == ROWS1_STEP:
                    use = G * (s + 1)
                    max_rows(0, use, M_BANK + use % NM, 1)
            iteration(0, 0, 0, first=True)
            with pe.Fori(0, NIT // 2 - 1) as u:
                iteration(2 * u + 1, 1, u)
                iteration(2 * u + 2, 0, u + 1)
            iteration(NIT - 1, 1, NIT // 2 - 1, last=True)
            pv_step(NIT - 1, 1, NS - 1)

        @block.vector
        def _(dve):
            def max_of_tile(s, j, use, bank):
                qt, kc = qtile(s)
                w = min(CH, (qt + 1) * P - kc * CH)
                dve.wait_ge(m_ready, use + 1)
                largest = part[:, qt // 8, j, qt % 8, kc:kc + 1]
                if kc == qt // TPC:
                    dve.sem_inc(masking, 1)
                    nc.vector.tensor_tensor_reduce(out=ps[:, bank, 0:w], in0=ps[:, bank, 0:w], in1=mask[:, CH - w:CH],
                                                   scale=1.0, scalar=MASKED, op0=ALU.add, op1=ALU.max,
                                                   accum_out=largest).then_inc(m_read, 1)
                else:
                    nc.vector.tensor_reduce(largest, ps[:, bank, 0:w], AX.X, ALU.max).then_inc(m_read, 1)

            def max_of_half(half, read):
                dve.wait_ge(m_read, read)
                nc.vector.tensor_reduce(qmax[:, half, :], part[:, half].rearrange("p j q k -> p (j q) k"), AX.X, ALU.max
                                        ).then_inc(qmax_done, 1)

            def rows_out(i, half, use, bank):
                dve.wait_ge(m_ready, use + 1)
                dve.wait_ge(rows_in[half], 16 * G * i)
                nc.vector.tensor_scalar(nrow[:, half, :], ps[0:G * 8, bank, 0:P], -1.0 / SQK, None, ALU.mult
                                        ).then_inc(m_read, 1)

            def turn(i, c):
                dve.wait_ge(o_copied, NC * i + c + 1)
                nc.vector.transpose(ot[:, c % 2].rearrange("p b r -> p (b r)"), o_sb[:, c % 2]).then_inc(ot_done, 1)

            def invert_sums(i, c):
                dve.wait_ge(ot_done, NC * i + c + 1)
                nc.vector.reciprocal(rsum[:, c % 2, :], ot[:, c % 2, :, DK]).then_inc(rsum_done, 1)

            def turn_back(i, c):
                dve.wait_ge(yt_done, NC * i + c + 1)
                nc.vector.transpose(y_sb[:, c % 2], yt[:, c % 2].rearrange("p b r -> p (b r)")).then_inc(y_done, 1)

            def iteration(i, p, first=False, last=False):
                for s in range(NS):
                    for j in range(G):
                        if not last:
                            max_of_tile(s, j, m_use(i, s, j), m_bank(p, s, j))
                        if j == 1:
                            for c in range(NC):
                                if s == TURN_STEP[c] + 1 and not (first and c == LATE):
                                    invert_sums(i - (c == LATE), c)
                    if s == ROWS2_STEP - 1:
                        max_of_half(1, NM + M_BEFORE + i * M_ITER)
                    if s == ROWS2_STEP:
                        rows_out(i, 1, second_rows_use(i, last), second_rows_bank(p, last))
                    if s == HALF_STEP and not last:
                        max_of_half(0, NM + m_use(i, HALF_STEP, 0))
                    if s == ROWS1_STEP and not last:
                        rows_out(i + 1, 0, rows_use(i, 0), rows_bank(p, 0))
                    for c in range(NC):
                        if first and c == LATE:
                            continue
                        if s == TURN_STEP[c]:
                            turn(i - (c == LATE), c)
                        if s == TURN_STEP[c] + BACK:
                            turn_back(i - (c == LATE), c)

            dve.sem_inc(m_read, NM)
            nc.vector.memset(part[:], -3e38).then_inc(part_preset, 1)
            dve.wait_ge(ops.const_in, 16)
            dve.wait_ge(part_preset, 1)
            for s in range(NS):
                for j in range(G):
                    use = G * s + j + (s > ROWS1_STEP)
                    max_of_tile(s, j, use, M_BANK + use % NM)
                if s == HALF_STEP:
                    max_of_half(0, NM + G * HALF_STEP)
                if s == ROWS1_STEP:
                    use = G * (s + 1)
                    rows_out(0, 0, use, M_BANK + use % NM)
            iteration(0, 0, first=True)
            with dve.Fori(0, NIT // 2 - 1) as u:
                iteration(2 * u + 1, 1)
                iteration(2 * u + 2, 0)
            iteration(NIT - 1, 1, last=True)
            turn(NIT - 1, LATE)
            invert_sums(NIT - 1, LATE)
            turn_back(NIT - 1, LATE)

        @block.scalar
        def _(act):
            def copy_o(i, c):
                act.wait_ge(pv_done, NS * i + CHUNK_END[c] + 1 + 2)
                act.wait_ge(ylo_done, NC * i + c + 1)
                nc.scalar.copy(o_sb[:, c % 2], ps[:, O_BANK]).then_inc(o_copied, 1)

            def y_split(i, c):
                act.wait_ge(y_done, NC * i + c + 1)
                act.wait_ge(y_out[c % 2], 32 * (2 * i + c // 2))
                nc.scalar.copy(y_hi[:, c % 2], y_sb[:, c % 2]).then_inc(yhi_done, 1)

            def iteration(i, first=False):
                for s in range(NS):
                    c, kb = STEPS[s]
                    q0 = max(0, kb - TPC * c) * P
                    act.wait_ge(pv_done, NS * i + s + 1)
                    for j in range(G):
                        act.wait_ge(s_ready, ST * i + G * s + j + 1)
                        nc.scalar.activation(prob[:, s % 2, j, q0:CH], ps[:, s_bank(s, j), q0:CH], ACT.Exp,
                                             scale=1.0 / (SQK * DK ** 0.5)).then_inc(p_done, 1)
                    if s == 0 and not first:
                        copy_o(i - 1, NC - 1)
                    for cc in range(NC):
                        if cc != LATE and s == CHUNK_END[cc] + 1:
                            copy_o(i, cc)
                        if s == TURN_STEP[cc] + SPLIT and not (first and cc == LATE):
                            y_split(i - (cc == LATE), cc)

            act.sem_inc(p_done, G)
            iteration(0, first=True)
            with act.Fori(0, NIT // 2 - 1) as u:
                iteration(2 * u + 1)
                iteration(2 * u + 2)
            iteration(NIT - 1)
            copy_o(NIT - 1, NC - 1)
            y_split(NIT - 1, NC - 1)

        @block.gpsimd
        def _(pool):
            pool.sem_inc(pv_done, 2)
            pool.sem_inc(ylo_done, 2)

            def mask_step(i, s):
                c, kb = STEPS[s]
                q0 = (kb - TPC * c) * P
                for j in range(G):
                    block = prob[:, s % 2, j, q0:q0 + P]
                    pool.wait_ge(p_done, ST * i + G * s + j + 1 + G)
                    pool.sem_inc(selecting, 1)
                    nc.gpsimd.affine_select(out=block, in_=block, compare_op=ALU.is_ge, fill=0.0, base=0,
                                            pattern=[[1, P]], channel_multiplier=-1).then_inc(mask_done, 1)

            def divide(i, c):
                pool.wait_ge(rsum_done, NC * i + c + 1)
                nc.gpsimd.tensor_tensor(yt[:, c % 2], ot[:, c % 2],
                                        rsum[:, c % 2, :].unsqueeze(2).to_broadcast([P, CH // 32, 32]), ALU.mult
                                        ).then_inc(yt_done, 1)

            def y_split(i, c):
                pool.wait_ge(yhi_done, NC * i + c + 1)
                nc.gpsimd.tensor_tensor(y_lo[:, c % 2], y_sb[:, c % 2], y_hi[:, c % 2], ALU.subtract).then_inc(ylo_done, 1)

            def iteration(i, first=False):
                for s in range(NS):
                    if is_diagonal(s):
                        mask_step(i, s)
                    for c in range(NC):
                        if first and c == LATE:
                            continue
                        if s == TURN_STEP[c] + 1:
                            divide(i - (c == LATE), c)
                        if s == TURN_STEP[c] + SPLIT:
                            y_split(i - (c == LATE), c)

            pool.wait_ge(w_in, 16 * len(w_f))
            for q, (f, (hi, lo)) in enumerate(zip(w_f, weights)):
                flat = "p k n -> p (k n)"
                f, hi, lo = f[:].rearrange(flat), hi[:].rearrange(flat), lo[:].rearrange(flat)
                nc.gpsimd.tensor_scalar(f, f, SX, None, ALU.mult).then_inc(w_scaled, 1)
                pool.wait_ge(w_scaled, q + 1)
                nc.gpsimd.tensor_copy(hi, f).then_inc(whi_done, 1)
                pool.wait_ge(whi_done, q + 1)
                nc.gpsimd.tensor_tensor(lo, f, hi, ALU.subtract).then_inc(w_done, 1)
            iteration(0, first=True)
            with pool.Fori(1, NIT) as i:
                iteration(i)
            divide(NIT - 1, NC - 1)
            y_split(NIT - 1, NC - 1)


def stage3(nc, x, att_d, weights, b1, b2, out, ops):
    with ExitStack() as ctx:
        def sb(name, shape, dt):
            return ctx.enter_context(nc.sbuf_tensor(name, shape, dt))

        def sem(name):
            return ctx.enter_context(nc.semaphore(name))

        (wo_hi, wo_lo), (w1_hi, w1_lo), (w2_hi, w2_lo) = weights
        b1_in = sb("s3_b1_in", [P, KF], F32)
        b1_s = sb("s3_b1_s", [P, KF], F32)
        b2_all = sb("s3_b2_all", [P, D], F32)
        eps = sb("s3_eps", [P, 1], F32)
        ident, xin, att_hi, att_lo, x_in, att_in = ops.ident, ops.xin, ops.att_hi, ops.att_lo, ops.x_in, ops.att_in
        x2 = sb("s3_x2", [P, 2, TPC, D], F32)
        x2b = sb("s3_x2b", [P, 2, TPC, D], F32)
        xn = sb("s3_xn", [P, 2, TPC, D], F32)
        stats = sb("s3_stats", [P, 2, TPC, 6], F32)
        mv = sb("s3_mv", [P, 2, TPC, 2], F32)
        std = sb("s3_std", [P, 2, TPC], F32)
        rstd = sb("s3_rstd", [P, 2, TPC], F32)
        xt_hi, xt_lo = sb("s3_xt_hi", [P, 2, KD, CH], F16), sb("s3_xt_lo", [P, 2, KD, CH], F16)
        h_f = sb("s3_h_f", [P, 2, CH], F32)
        h_hi, h_lo = sb("s3_h_hi", [P, 2, KF, CH], F16), sb("s3_h_lo", [P, 2, KF, CH], F16)
        y = sb("s3_y", [P, 2, TPC, D], F32)
        ps = ctx.enter_context(nc.psum_tensor("s3_ps", [P, 8, CH], F32))
        A_BANK, XT_BANK, H_BANK, Y_BANK = 0, 2, 4, 6

        w_in, preset, aggregating = sem("s3_w_in"), sem("s3_preset"), sem("s3_aggregating")
        a_ready, x2_done, x2b_done = sem("s3_a_ready"), sem("s3_x2_done"), sem("s3_x2b_done")
        stats_done, mv_done, std_done = sem("s3_stats_done"), sem("s3_mv_done"), sem("s3_std_done")
        rstd_done, xn_done = sem("s3_rstd_done"), sem("s3_xn_done")
        xt_ready, xhi_done, xlo_done = sem("s3_xt_ready"), sem("s3_xhi_done"), sem("s3_xlo_done")
        h_ready, h_done, hhi_done, hlo_done = sem("s3_h_ready"), sem("s3_h_done"), sem("s3_hhi_done"), sem("s3_hlo_done")
        y_ready, y_done = sem("s3_y_ready"), sem("s3_y_done")
        y_out = [sem(f"s3_y_out{p}") for p in range(2)]
        NPAIR = NCHUNK // 2

        block = ctx.enter_context(nc.Block())

        @block.sync
        def _(sp):
            def step(b, cc, last):
                n, p = NC * b + cc, cc % 2
                if not (last and cc >= NC - 2):
                    sp.wait_ge(x2_done, 2 * (n + 1) + 2)
                    load_x(sp, ops, x, n + 2, p)
                    if cc + 2 < NC:
                        load_att(sp, ops, att_d, b, cc + 2, p)
                    else:
                        load_att(sp, ops, att_d, b + 1, cc + 2 - NC, p)
                for pair in range(2):
                    sp.wait_ge(y_done, 2 * n + pair + 1 + 2)
                    sp.dma_start(out[bass.ds(n * CH + pair * 2 * P, 2 * P), :].rearrange("(t p) d -> p t d", p=P),
                                 y[:, p, 2 * pair:2 * pair + 2]).then_inc(y_out[p], 16)

            sp.dma_start(b1_in[:], b1).then_inc(w_in, 16)
            sp.dma_start(b2_all[:], b2.rearrange("(a d) -> a d", a=1).to_broadcast([P, D])).then_inc(w_in, 16)
            with sp.Fori(0, B - 1) as b:
                for cc in range(NC):
                    step(b, cc, False)
            for cc in range(NC):
                step(B - 1, cc, True)
            for p in range(2):
                sp.wait_ge(y_out[p], 32 * (NPAIR + 1))

        @block.tensor
        def _(pe):
            def project(n, p, use):
                pe.wait_ge(att_in[p], 16 * 2 * NG * (use + 1))
                for pair in range(2):
                    pe.wait_ge(x2_done, 2 * n + pair + 1)
                    for t in range(2):
                        tt = 2 * pair + t
                        mm = [(a, w, k) for a, w in terms(att_hi, att_lo, wo_hi, wo_lo) for k in range(KD)]
                        for q, (a, w, k) in enumerate(mm):
                            last = nc.tensor.matmul(ps[:, A_BANK + pair, t * D:(t + 1) * D],
                                                    a[:, p, k, tt * P:(tt + 1) * P], w[:, k],
                                                    start=q == 0, stop=q == len(mm) - 1)
                    last.then_inc(a_ready, 1)

            def transposes(n, p):
                pe.wait_ge(xn_done, n + 1)
                pe.wait_ge(xlo_done, n)
                for k in range(KD):
                    for t in range(TPC):
                        last = nc.tensor.transpose(ps[:, XT_BANK + k, t * P:(t + 1) * P],
                                                   xn[:, p, t, k * P:(k + 1) * P], ident[:])
                last.then_inc(xt_ready, 1)

            def ffn1(n, p):
                pe.wait_ge(xlo_done, n + 1)
                for f in range(KF):
                    pe.wait_ge(h_done, KF * n + f + 1)
                    mm = [(w, a, k) for w, a in terms(w1_hi, w1_lo, xt_hi, xt_lo) for k in range(KD)]
                    for q, (w, a, k) in enumerate(mm):
                        last = nc.tensor.matmul(ps[:, H_BANK + f % 2], w[:, k, f * P:(f + 1) * P], a[:, p, k],
                                                start=q == 0, stop=q == len(mm) - 1)
                    last.then_inc(h_ready, 1)

            def ffn2_tile(n, p, tt):
                pair, t = divmod(tt, 2)
                if t == 0:
                    pe.wait_ge(y_done, 2 * n + pair + 1)
                mm = [(a, w, k) for k in range(KF) for a, w in terms(h_hi, h_lo, w2_hi, w2_lo)]
                for q, (a, w, k) in enumerate(mm):
                    last = nc.tensor.matmul(ps[:, Y_BANK + pair, t * D:(t + 1) * D],
                                            a[:, p, k, tt * P:(tt + 1) * P], w[:, k],
                                            start=q == 0, stop=q == len(mm) - 1)
                if t == 1:
                    last.then_inc(y_ready, 1)

            def step(n, p, next_use, last=False):
                ffn1(n, p)
                if not last:
                    project(n + 1, 1 - p, next_use)
                pe.wait_ge(hlo_done, KF * (n + 1) + 2)
                for tt in range(TPC):
                    if tt == TPC - 1 and not last:
                        transposes(n + 1, 1 - p)
                    ffn2_tile(n, p, tt)

            project(0, 0, 0)
            transposes(0, 0)
            with pe.Fori(0, NPAIR - 1) as u:
                step(2 * u, 0, u)
                step(2 * u + 1, 1, u + 1)
            step(NCHUNK - 2, 0, NPAIR - 1)
            step(NCHUNK - 1, 1, 0, last=True)

        @block.vector
        def _(dve):
            def residual(n, p, use):
                dve.wait_ge(x_in[p], 16 * (use + 1))
                for pair in range(2):
                    dve.wait_ge(a_ready, 2 * n + pair + 1)
                    dve.wait_ge(x2b_done, n + 1)
                    nc.vector.scalar_tensor_tensor(x2[:, p, 2 * pair:2 * pair + 2].rearrange("p t d -> p (t d)"),
                                                   ps[:, A_BANK + pair], 1.0 / SQK,
                                                   xin[:, p, 2 * pair:2 * pair + 2].rearrange("p t d -> p (t d)"),
                                                   ALU.mult, ALU.add).then_inc(x2_done, 1)

            def statistics(n, p):
                dve.wait_ge(x2_done, 2 * (n + 1) + 2)
                for t in range(TPC):
                    nc.vector.bn_stats(stats[:, p, t, :], x2[:, p, t, :]).then_inc(stats_done, 1)

            def normalize(n, p):
                dve.wait_ge(stats_done, TPC * (n + 1))
                dve.sem_inc(aggregating, 1)
                for t in range(TPC):
                    last = nc.vector.bn_aggr(mv[:, p, t, :], stats[:, p, t, :])
                last.then_inc(mv_done, 1)
                dve.wait_ge(std_done, n + 1)
                nc.vector.reciprocal(rstd[:, p, :], std[:, p, :]).then_inc(rstd_done, 1)
                dve.wait_ge(rstd_done, n + 1)
                for t in range(TPC):
                    last = nc.vector.tensor_scalar(xn[:, p, t, :], x2[:, p, t, :], mv[:, p, t, 0:1],
                                                   rstd[:, p, t:t + 1], ALU.subtract, ALU.mult)
                last.then_inc(xn_done, 1)

            def split_xt(n, p):
                dve.wait_ge(xhi_done, n + 1)
                for k in range(KD):
                    last = nc.vector.tensor_tensor(xt_lo[:, p, k], ps[:, XT_BANK + k], xt_hi[:, p, k], ALU.subtract)
                last.then_inc(xlo_done, 1)

            def split_h(n, p, f):
                dve.wait_ge(h_done, KF * n + f + 1 + 2)
                nc.vector.tensor_copy(h_hi[:, p, f], h_f[:, f % 2]).then_inc(hhi_done, 1)
                dve.wait_ge(hhi_done, KF * n + f + 1)
                nc.vector.tensor_tensor(h_lo[:, p, f], h_f[:, f % 2], h_hi[:, p, f], ALU.subtract).then_inc(hlo_done, 1)

            def output(n, p, use, pair):
                dve.wait_ge(y_ready, 2 * n + pair + 1)
                dve.wait_ge(x2b_done, n + 1 + 2)
                dve.wait_ge(y_out[p], 32 * (use + 1))
                nc.vector.scalar_tensor_tensor(y[:, p, 2 * pair:2 * pair + 2].rearrange("p t d -> p (t d)"),
                                               ps[:, Y_BANK + pair], 1.0 / (SH * SX),
                                               x2b[:, p, 2 * pair:2 * pair + 2].rearrange("p t d -> p (t d)"),
                                               ALU.mult, ALU.add).then_inc(y_done, 1)

            def step(n, p, use, next_use, last=False):
                for f in range(KF):
                    split_h(n, p, f)
                if not last:
                    residual(n + 1, 1 - p, next_use)
                    statistics(n + 1, 1 - p)
                    normalize(n + 1, 1 - p)
                output(n, p, use, 0)
                if not last:
                    split_xt(n + 1, 1 - p)
                output(n, p, use, 1)

            dve.sem_inc(x2b_done, 2)
            dve.sem_inc(y_done, 2)
            for p in range(2):
                dve.sem_inc(y_out[p], 32)
            dve.sem_inc(x2_done, 2)
            dve.sem_inc(hlo_done, 2)
            nc.vector.memset(eps[:], EPS / SX ** 2).then_inc(preset, 1)
            dve.wait_ge(w_in, 32)
            nc.vector.tensor_scalar(b1_s[:], b1_in[:], SH, None, ALU.mult).then_inc(preset, 1)
            residual(0, 0, 0)
            statistics(0, 0)
            normalize(0, 0)
            split_xt(0, 0)
            with dve.Fori(0, NPAIR - 1) as u:
                step(2 * u, 0, u, u)
                step(2 * u + 1, 1, u, u + 1)
            step(NCHUNK - 2, 0, NPAIR - 1, NPAIR - 1)
            step(NCHUNK - 1, 1, NPAIR - 1, 0, last=True)

        @block.scalar
        def _(act):
            def std_of(n, p):
                act.wait_ge(mv_done, n + 1)
                nc.scalar.activation(std[:, p, :], mv[:, p, :, 1], ACT.Sqrt, bias=eps[:], scale=1.0 / SX ** 2
                                     ).then_inc(std_done, 1)

            def hi_xt(n, p):
                act.wait_ge(xt_ready, n + 1)
                for k in range(KD):
                    last = nc.scalar.copy(xt_hi[:, p, k], ps[:, XT_BANK + k])
                last.then_inc(xhi_done, 1)

            def relu(n, f):
                act.wait_ge(h_ready, KF * n + f + 1)
                act.wait_ge(hlo_done, KF * n + f + 1)
                nc.scalar.activation(h_f[:, f % 2], ps[:, H_BANK + f % 2], ACT.Relu, bias=b1_s[:, f:f + 1],
                                     scale=SH / SQK).then_inc(h_done, 1)

            def step(n, p, last=False):
                for f in range(KF):
                    relu(n, f)
                if not last:
                    std_of(n + 1, 1 - p)
                    hi_xt(n + 1, 1 - p)

            act.sem_inc(h_done, 2)
            act.wait_ge(preset, 2)
            std_of(0, 0)
            hi_xt(0, 0)
            with act.Fori(0, NPAIR - 1) as u:
                step(2 * u, 0)
                step(2 * u + 1, 1)
            step(NCHUNK - 2, 0)
            step(NCHUNK - 1, 1, last=True)

        @block.gpsimd
        def _(pool):
            def add_b2(n, p):
                pool.wait_ge(x2_done, 2 * (n + 1) + 2)
                if not isinstance(n, int) or n > 1:
                    pool.wait_ge(y_done, 2 * n)
                for t in range(TPC):
                    last = nc.gpsimd.tensor_tensor(x2b[:, p, t], x2[:, p, t], b2_all[:], ALU.add)
                last.then_inc(x2b_done, 1)

            pool.wait_ge(w_in, 32)
            add_b2(0, 0)
            add_b2(1, 1)
            with pool.Fori(1, NPAIR) as u:
                add_b2(2 * u, 0)
                add_b2(2 * u + 1, 1)


def layer(nc, x, wqkv, wo, w1, b1, w2, b2, cos_d, sin_d, ident_d, mask_d, out):
    qk_d = nc.dram_tensor("qk_scratch", (NIT, 2, 2, GC, S), F16, kind="Internal").ap()
    v_d = nc.dram_tensor("v_scratch", (P, S // P, NIT, G * 2 * DK), F32, kind="Internal").ap()
    att_d = nc.dram_tensor("att_scratch", (2, NIT, P, S), F16, kind="Internal").ap()
    with ExitStack() as ctx:
        weights = [[ctx.enter_context(nc.sbuf_tensor(f"{name}_{part}", [P, k, n], F16)) for part in ("hi", "lo")]
                   for name, k, n in (("wo", KD, D), ("w1", KD, F), ("w2", KF, D))]
        with ExitStack() as attention:
            ops = Operands(nc, attention)
            stage1(nc, x, wqkv, cos_d, sin_d, ident_d, mask_d, qk_d, v_d, ops)
            stage2(nc, x, qk_d, v_d, att_d, (wo, w1, w2), weights, ops)
            stage3(nc, x, att_d, weights, b1, b2, out, ops)


def shape_constants():
    freqs = (1.0 / np.float32(10000.0) ** (np.arange(0, DK, 2, dtype=np.float32) / np.float32(DK))).astype(np.float32)
    angles = freqs[(np.arange(P) % DK) // 2][:, None] * np.arange(S, dtype=np.float32)[None, :]
    sign = np.where(np.arange(P) % 2 == 0, -1.0, 1.0)[:, None]
    cos = (np.cos(angles) / SX).astype(np.float32)
    sin = (np.sin(angles) * sign / SX).astype(np.float32)
    r = np.arange(P)
    mask = np.concatenate([np.zeros((P, CH - P)), np.where(r[None, :] > r[:, None], MASKED, 0.0)], axis=1)
    return {"cos": cos, "sin": sin, "ident": np.eye(P, dtype=np.float32), "mask": mask.astype(np.float32)}


def kernel(L0_attn_x, L0_attn_Wq, L0_attn_Wk, L0_attn_Wv, L0_attn_Wo, L0_ffn_w1, L0_ffn_b1, L0_ffn_w2, L0_ffn_b2):
    import concourse.bacc as bacc
    from concourse.bass_utils import run_bass_kernel_spmd

    wq, wk, wv, wo = (np.asarray(w).T for w in (L0_attn_Wq, L0_attn_Wk, L0_attn_Wv, L0_attn_Wo))
    cols = []
    for g in range(NG):
        cols += [wq[:, GC * g:GC * (g + 1)], wk[:, GC * g:GC * (g + 1)]]
    arrays = {
        "x": np.asarray(L0_attn_x).reshape(B * S, D),
        "w_qkv": np.concatenate(cols + [wv], axis=1),
        "w_o": wo,
        "w_1": np.asarray(L0_ffn_w1), "b_1": np.asarray(L0_ffn_b1).reshape(KF, P).T,
        "w_2": np.asarray(L0_ffn_w2), "b_2": np.asarray(L0_ffn_b2),
        **shape_constants(),
    }
    arrays = {name: np.ascontiguousarray(a) for name, a in arrays.items()}
    nc = bacc.Bacc("TRN2", target_bir_lowering=False, num_devices=1)
    args = [nc.dram_tensor(name, a.shape, mybir.dt.from_np(a.dtype), kind="ExternalInput").ap()
            for name, a in arrays.items()]
    out = nc.dram_tensor("out", (B * S, D), F32, kind="ExternalOutput").ap()
    layer(nc, *args, out)
    r = run_bass_kernel_spmd(nc, [arrays], core_ids=[0])
    return r.results[0]["out"].reshape(B, S, D)
```
